# Optimizing a Trainium2 kernel written in Bass

```python
import numpy as np
import jax
import jax.numpy as jnp

def _softmax(x, axis=-1):
    return jax.nn.softmax(x, axis=axis)

def _gelu(x):
    return jax.nn.gelu(x, approximate=True)

def _silu(x):
    return jax.nn.silu(x)

def _sigmoid(x):
    return jax.nn.sigmoid(x)

def _layernorm(x, axis=-1, eps=1e-05):
    m = jnp.mean(x, axis=axis, keepdims=True)
    v = jnp.var(x, axis=axis, keepdims=True)
    return (x - m) / jnp.sqrt(v + eps)

def _scatter_add(tgt, idx, src, axis=0):
    return tgt.at[idx].add(src)

def _segment_sum(src, seg, n):
    return jax.ops.segment_sum(src, seg, n)
kernel_name = 'mk_xattn_ffn_d1_seqx_r8_6cc037'

def setup_inputs(seed: int=0):
    np.random.seed(seed)
    _w = jnp.asarray

    def _rec_inputs():
        import jax
        import jax.numpy as jnp
        _rk = jax.random.key(seed)
        x = -0.000125 + 0.9999 * jax.random.normal(jax.random.fold_in(_rk, 1), (32, 64, 256), jnp.float32)
        _lenS = 64 - jax.random.randint(jax.random.fold_in(_rk, 7), (32,), 0, max(1, 64 // 4) + 1, jnp.int32)
        _lenS2 = 64 - jax.random.randint(jax.random.fold_in(_rk, 8), (32,), 0, max(1, 64 // 4) + 1, jnp.int32)
        _ctx_2048P = jax.random.normal(jax.random.fold_in(_rk, 11), (32, 16, 256), jnp.float32)
        _ctx_2048c = jax.random.dirichlet(jax.random.fold_in(_rk, 511), 0.3 * jnp.ones((16,), jnp.float32), (32, 64))
        _ctx_2048t = jnp.einsum('bsk,bkd->bsd', _ctx_2048c, _ctx_2048P)
        _ctx_2048t = _ctx_2048t * jax.lax.rsqrt(jnp.mean(jnp.square(_ctx_2048t)) + 1e-12) * 0.953939
        ctx_2048 = -0.000514642 + 1.00011 * (_ctx_2048t + 0.3 * jax.random.normal(jax.random.fold_in(_rk, 611), (32, 64, 256), jnp.float32))
        _validS = jnp.arange(64)[None, :] < _lenS[:, None]
        _validS2 = jnp.arange(64)[None, :] < _lenS2[:, None]
        _causal = jnp.tril(jnp.ones((64, 64), dtype=bool))
        mask_BxS2_bk0 = jnp.logical_not(jnp.broadcast_to(_validS2[:, :], (32, 64)))
        return (x, ctx_2048, mask_BxS2_bk0)
    x, ctx_2048, mask_BxS2_bk0 = _rec_inputs()

    def _L0_xattn_setup():
        import jax, jax.numpy as jnp
        import numpy as np
        key = jax.random.key(seed)
        k1, k2, k3 = jax.random.split(key, 3)
        B, S, D, M = (8, 256, 256, 128)
        hidden_states = jax.random.normal(k1, (B, S, D), dtype=jnp.float32)
        memory_tokens = jax.random.normal(k2, (B, M, D), dtype=jnp.float32)
        memory_mask = jax.random.randint(k3, (B, M), 0, 2).astype(jnp.bool_)
        return {'hidden_states': hidden_states, 'memory_tokens': memory_tokens, 'memory_mask': memory_mask}
    _L0_xattn_all = _L0_xattn_setup()
    _L0_xattn_in = {k: v for k, v in _L0_xattn_all.items() if k in ()}
    del _L0_xattn_all

    def _L0_ffn_setup():
        import jax, jax.numpy as jnp
        import numpy as np
        H = 256
        key = jax.random.key(seed)
        ks = jax.random.split(key, 10)
        s = 1.0 / np.sqrt(H)
        x = jax.random.normal(ks[0], (4, 256, H), dtype=jnp.float32)
        Wg = jax.random.uniform(ks[1], (2, H), jnp.float32, -s, s)
        W0a = jax.random.uniform(ks[2], (2 * H, H), jnp.float32, -s, s)
        b0a = jax.random.uniform(ks[3], (2 * H,), jnp.float32, -s, s)
        W0b = jax.random.uniform(ks[4], (H, 2 * H), jnp.float32, -s, s)
        b0b = jax.random.uniform(ks[5], (H,), jnp.float32, -s, s)
        W1a = jax.random.uniform(ks[6], (2 * H, H), jnp.float32, -s, s)
        b1a = jax.random.uniform(ks[7], (2 * H,), jnp.float32, -s, s)
        W1b = jax.random.uniform(ks[8], (H, 2 * H), jnp.float32, -s, s)
        b1b = jax.random.uniform(ks[9], (H,), jnp.float32, -s, s)
        return {'x': x, 'Wg': Wg, 'W0a': W0a, 'b0a': b0a, 'W0b': W0b, 'b0b': b0b, 'W1a': W1a, 'b1a': b1a, 'W1b': W1b, 'b1b': b1b}
    _L0_ffn_all = _L0_ffn_setup()
    _L0_ffn_in = {k: v for k, v in _L0_ffn_all.items() if k in ('Wg', 'W0a', 'b0a', 'W0b', 'b0b', 'W1a', 'b1a', 'W1b', 'b1b')}
    del _L0_ffn_all
    return {'x': x, 'ctx_2048': ctx_2048, 'mask_BxS2_bk0': mask_BxS2_bk0, 'L0_ffn_Wg': _L0_ffn_in['Wg'], 'L0_ffn_W0a': _L0_ffn_in['W0a'], 'L0_ffn_b0a': _L0_ffn_in['b0a'], 'L0_ffn_W0b': _L0_ffn_in['W0b'], 'L0_ffn_b0b': _L0_ffn_in['b0b'], 'L0_ffn_W1a': _L0_ffn_in['W1a'], 'L0_ffn_b1a': _L0_ffn_in['b1a'], 'L0_ffn_W1b': _L0_ffn_in['W1b'], 'L0_ffn_b1b': _L0_ffn_in['b1b']}

def reference(x, ctx_2048, mask_BxS2_bk0, L0_ffn_Wg, L0_ffn_W0a, L0_ffn_b0a, L0_ffn_W0b, L0_ffn_b0b, L0_ffn_W1a, L0_ffn_b1a, L0_ffn_W1b, L0_ffn_b1b):
    import jax
    import jax.numpy as jnp

    def _L0_xattn_ref(hidden_states, memory_tokens, memory_mask):
        import jax, jax.numpy as jnp
        import numpy as np
        B, S, D = hidden_states.shape
        scale = 1.0 / jnp.sqrt(jnp.asarray(D, hidden_states.dtype))
        scores = jnp.einsum('bsd,bmd->bsm', hidden_states, memory_tokens) * scale
        neg_inf = jnp.asarray(-1e+30, scores.dtype)
        scores = jnp.where(memory_mask[:, None, :], scores, neg_inf)
        attn = jax.nn.softmax(scores, axis=-1)
        readout = jnp.einsum('bsm,bmd->bsd', attn, memory_tokens)
        valid_b = jnp.any(memory_mask, axis=-1)
        out = jnp.where(valid_b[:, None, None], readout, jnp.zeros_like(readout))
        return out

    def _L0_ffn_ref(x, Wg, W0a, b0a, W0b, b0b, W1a, b1a, W1b, b1b):
        import jax, jax.numpy as jnp
        import numpy as np
        H = 256
        scores = jax.nn.softmax(jnp.einsum('bsh,eh->bse', x, Wg), axis=-1)
        top_expert = jnp.argmax(scores, axis=-1)
        h0 = jax.nn.gelu(jnp.einsum('bsh,fh->bsf', x, W0a) + b0a, approximate=False)
        out0 = jnp.einsum('bsf,hf->bsh', h0, W0b) + b0b
        h1 = jax.nn.relu(jnp.einsum('bsh,fh->bsf', x, W1a) + b1a)
        out1 = jnp.einsum('bsf,hf->bsh', h1, W1b) + b1b
        mask0 = (top_expert == 0).astype(x.dtype)[..., None]
        return out0 * mask0 + out1 * (1.0 - mask0)
    x = x + _L0_xattn_ref(_layernorm(x, axis=-1), ctx_2048, mask_BxS2_bk0)
    x = x + _L0_ffn_ref(_layernorm(x, axis=-1), L0_ffn_Wg, L0_ffn_W0a, L0_ffn_b0a, L0_ffn_W0b, L0_ffn_b0b, L0_ffn_W1a, L0_ffn_b1a, L0_ffn_W1b, L0_ffn_b1b)
    return x

_drawn_inputs = setup_inputs


def setup_inputs(seed=0):
    import zlib

    import numpy as np

    out = dict(_drawn_inputs(seed))
    spreads = {}
    factors = {'L0_ffn_b0a': 6.056, 'L0_ffn_b0b': 2.859, 'L0_ffn_b1a': 4.9, 'L0_ffn_b1b': 2.689}
    for name, (base, spread) in spreads.items():
        noise = np.random.default_rng([zlib.crc32(name.encode()), seed]).standard_normal(out[name].shape)
        drawn = base * np.exp(spread * noise) if base else spread * noise
        out[name] = jnp.asarray(drawn.astype(out[name].dtype))
    for name, factor in factors.items():
        out[name] = (out[name] * factor).astype(out[name].dtype)
    return out
```

```python
from contextlib import ExitStack

import concourse.bass as bass
from concourse import mybir

P = 128
B, S, D = 32, 64, 256
F = 512
E = 2
TILES = 2
GROUP = TILES * P
GROUPS = B * S // GROUP
KC = D // P
FC = E * F // P
CS = 2
STEPS = FC // CS
LAG = 2
NEG = -1e30
EPS = 1e-5

ALU = mybir.AluOpType
ACT = mybir.ActivationFunctionType
F32 = mybir.dt.float32
F32R = mybir.dt.float32r
U8 = mybir.dt.uint8
AX_X = mybir.AxisListType.X


class Group:

    def __init__(self, pair, offset):
        self.pair, self.offset = pair, offset
        self.n = pair * 2 + offset
        self.buf = offset % 2
        self.turn = pair + offset // 2

    def __add__(self, k):
        return Group(self.pair, self.offset + k)


def xattn_ffn(nc, x, ctx, ctx_t, mask, gate_w, w_in, b_in, w_out, b_out, out):
    x_tok = x.rearrange("(g t p) d -> g p t d", t=TILES, p=P)
    out_tok = out.rearrange("(g t p) d -> g p t d", t=TILES, p=P)

    with ExitStack() as stack:
        def sb(name, shape, dt=F32):
            return stack.enter_context(nc.sbuf_tensor(name, shape, dt))

        def bank(name):
            return stack.enter_context(nc.psum_tensor(name, [P, 512], F32))

        def sem(name):
            return stack.enter_context(nc.semaphore(name))

        ident = sb("ident", [P, P])
        minus_half = sb("minus_half", [P, TILES])
        mask_u8 = sb("mask_u8", [P, B // 2, S], U8)
        penalty = sb("penalty", [P, B // 2, S])
        gate_rows = sb("gate_rows", [P, E, D])
        gate_diff = sb("gate_diff", [P, D])
        b_in_sb = sb("b_in_sb", [P, FC])
        b_out_sb = sb("b_out_sb", [P, E, D])
        wi = sb("wi", [P, KC, E * F])
        wi_hi = sb("wi_hi", [P, KC, E * F], F32R)
        wi_lo = sb("wi_lo", [P, KC, E * F], F32R)
        wo = sb("wo", [P, FC, D])
        wo_hi = sb("wo_hi", [P, FC, D], F32R)
        wo_lo = sb("wo_lo", [P, FC, D], F32R)
        x_sb = sb("x_sb", [P, 2, TILES, D])
        ctx_t_sb = sb("ctx_t_sb", [P, 2, KC, 4 * S])
        ctx_sb = sb("ctx_sb", [P, 2, 2, D])
        stats = sb("stats", [P, TILES, 6])
        mean_var = sb("mean_var", [P, TILES, 2])
        var_eps = sb("var_eps", [P, TILES])
        rstd = sb("rstd", [P, TILES])
        xn = sb("xn", [P, TILES, D])
        xn_t = sb("xn_t", [P, TILES, KC, P])
        masked = sb("masked", [P, TILES, S])
        row_max = sb("row_max", [P, TILES])
        centred = sb("centred", [P, TILES, S])
        probs = sb("probs", [P, TILES, S])
        probs_t = sb("probs_t", [P, P])
        row_sum = sb("row_sum", [P, TILES])
        row_inv = sb("row_inv", [P, TILES])
        row_scale = sb("row_scale", [P, TILES])
        x2 = sb("x2", [P, TILES, D])
        stats2 = sb("stats2", [P, TILES, 6])
        mean_var2 = sb("mean_var2", [P, TILES, 2])
        var_eps2 = sb("var_eps2", [P, TILES])
        rstd2 = sb("rstd2", [P, TILES])
        x2n = sb("x2n", [P, TILES, D])
        x2t_hi = sb("x2t_hi", [P, 2, KC, GROUP], F32R)
        x2t_lo = sb("x2t_lo", [P, 2, KC, GROUP], F32R)
        gate_prod = sb("gate_prod", [P, TILES, D])
        gate_sum = sb("gate_sum", [P, TILES])
        chosen = sb("chosen", [P, 2, E, TILES])
        bias0 = sb("bias0", [P, TILES, D])
        bias1 = sb("bias1", [P, TILES, D])
        bias01 = sb("bias01", [P, TILES, D])
        base = sb("base", [P, 2, TILES, D])
        hid = sb("hid", [P, 2, CS, GROUP])
        hid_hi = sb("hid_hi", [P, STEPS, CS, GROUP], F32R)
        hid_lo = sb("hid_lo", [P, STEPS, CS, GROUP], F32R)
        part = sb("part", [P, TILES, D])
        out_sb = sb("out_sb", [P, 2, TILES, D])

        ps_hid = [bank(f"ps_hid{i}") for i in range(2)]
        ps_y = [bank(f"ps_y{e}") for e in range(E)]
        ps_read = [bank(f"ps_read{j}") for j in range(2)]
        ps_turn = bank("ps_turn")
        ps_score = bank("ps_score")
        ps_turn2 = ps_read[0]

        x_loaded = [sem(f"x_loaded{i}") for i in range(2)]
        ctx_t_loaded = [sem(f"ctx_t_loaded{i}") for i in range(2)]
        ctx_loaded = [sem(f"ctx_loaded{i}") for i in range(2)]
        stored = [sem(f"stored{i}") for i in range(2)]
        mask_loaded = sem("mask_loaded")
        rows_loaded = sem("rows_loaded")
        b_in_loaded = sem("b_in_loaded")
        wi_loaded = sem("wi_loaded")
        wo_loaded = sem("wo_loaded")
        ident_zero = sem("ident_zero")
        ident_ready = sem("ident_ready")
        half_ready = sem("half_ready")
        penalty_ready = sem("penalty_ready")
        gate_ready = sem("gate_ready")
        wi_hi_ready = sem("wi_hi_ready")
        wi_lo_ready = sem("wi_lo_ready")
        wo_hi_ready = sem("wo_hi_ready")
        wo_lo_ready = sem("wo_lo_ready")
        dve_passed, pe_passed, pool_passed = sem("dve_passed"), sem("pe_passed"), sem("pool_passed")
        stats_done = sem("stats_done")
        aggr_done = sem("aggr_done")
        var_done = sem("var_done")
        rstd_done = sem("rstd_done")
        xn_done = sem("xn_done")
        xn_turned = sem("xn_turned")
        xn_t_done = sem("xn_t_done")
        scores_done = sem("scores_done")
        masked_done = sem("masked_done")
        max_done = sem("max_done")
        centred_done = sem("centred_done")
        probs_done = sem("probs_done")
        probs_turned = sem("probs_turned")
        probs_t_done = sem("probs_t_done")
        sum_done = sem("sum_done")
        inv_done = sem("inv_done")
        scale_done = sem("scale_done")
        read_done = sem("read_done")
        x2_done = sem("x2_done")
        stats2_done = sem("stats2_done")
        aggr2_done = sem("aggr2_done")
        var2_done = sem("var2_done")
        rstd2_done = sem("rstd2_done")
        x2n_done = sem("x2n_done")
        x2_turned = sem("x2_turned")
        x2t_hi_done = sem("x2t_hi_done")
        x2t_lo_done = sem("x2t_lo_done")
        gate_done = sem("gate_done")
        chosen_done = sem("chosen_done")
        biased = sem("biased")
        bias_sum = sem("bias_sum")
        base_done = sem("base_done")
        part_done = sem("part_done")
        out_done = sem("out_done")
        hid_ready = sem("hid_ready")
        hid_taken = sem("hid_taken")
        hid_hi_done = sem("hid_hi_done")
        hid_lo_done = sem("hid_lo_done")
        second_done = sem("second_done")

        block = stack.enter_context(nc.Block())

        def run(engine, before, body):
            before()
            body(Group(0, 0), first=True)
            with engine.Fori(0, (GROUPS - 4) // 2) as pair:
                body(Group(pair, 1))
                body(Group(pair, 2))
            body(Group(0, GROUPS - 3))
            body(Group(0, GROUPS - 2), left=1)
            body(Group(0, GROUPS - 1), left=0)

        @block.sync
        def _(sp):
            def load_x(g, again=True):
                if again:
                    sp.wait_ge(x2_done, g.n - 1)
                sp.dma_start(x_sb[:, g.buf], x_tok[g.n]).then_inc(x_loaded[g.buf], 16)

            def load_ctx_t(g, again=True):
                if again:
                    sp.wait_ge(scores_done, g.n - 1)
                sp.dma_start(ctx_t_sb[:, g.buf], ctx_t[g.n]).then_inc(ctx_t_loaded[g.buf], 16)

            def load_ctx(g, again=True):
                if again:
                    sp.wait_ge(read_done, g.n - 1)
                sp.dma_start(ctx_sb[:, g.buf], ctx[g.n]).then_inc(ctx_loaded[g.buf], 16)

            def before():
                g0, g1 = Group(0, 0), Group(0, 1)
                load_x(g0, False)
                for h in range(2):
                    sp.dma_start(mask_u8[h * S:(h + 1) * S], mask[h:h + 1].to_broadcast([S, B // 2, S])
                                 ).then_inc(mask_loaded, 16)
                load_ctx_t(g0, False)
                load_ctx(g0, False)
                load_x(g1, False)
                sp.dma_start(wi[:, :, :], w_in).then_inc(wi_loaded, 16)
                sp.dma_start(gate_rows[:, :, :], gate_w.to_broadcast([P, E, D])).then_inc(rows_loaded, 16)
                sp.dma_start(b_out_sb[:, :, :], b_out.to_broadcast([P, E, D])).then_inc(rows_loaded, 16)
                sp.dma_start(b_in_sb[:, :], b_in).then_inc(b_in_loaded, 16)
                load_ctx_t(g1, False)
                sp.dma_start(wo[:, :, :], w_out).then_inc(wo_loaded, 16)
                load_ctx(g1, False)

            def store(g):
                sp.wait_ge(out_done, g.n + 1)
                sp.dma_start(out_tok[g.n], out_sb[:, g.buf]).then_inc(stored[g.buf], 16)

            def body(g, first=False, left=2):
                if left == 2:
                    load_x(g + 2, not first)
                    load_ctx_t(g + 2, not first)
                    load_ctx(g + 2, not first)
                if not first:
                    store(g + -1)

            def body_sp(g, first=False, left=2):
                if left == 2:
                    load_x(g + 2)
                    load_ctx_t(g + 2)
                if not first:
                    store(g + -1)
                if left == 2:
                    load_ctx(g + 2)

            run(sp, before, body_sp)
            store(Group(0, GROUPS - 1))
            for i in range(2):
                sp.wait_ge(stored[i], 16 * (GROUPS // 2))

        @block.gpsimd
        def _(pool):
            def first_norm(g):
                pool.wait_ge(var_done, g.n + 1)
                pool.tensor_tensor(rstd[:, :], var_eps[:, :], minus_half[:, :], ALU.pow).then_inc(rstd_done, 1)

            def second_norm(g):
                pool.wait_ge(var2_done, g.n + 1)
                pool.tensor_tensor(rstd2[:, :], var_eps2[:, :], minus_half[:, :], ALU.pow).then_inc(rstd2_done, 1)

            def residual(g):
                pool.wait_ge(chosen_done, g.n + 1)
                pool.sem_inc(pool_passed, 1)
                for t in range(TILES):
                    pool.tensor_scalar(bias0[:, t], b_out_sb[:, 0], chosen[:, g.buf, 0, t:t + 1], 0.0,
                                       ALU.mult, ALU.add)
                    last = pool.tensor_scalar(bias1[:, t], b_out_sb[:, 1], chosen[:, g.buf, 1, t:t + 1], 0.0,
                                              ALU.mult, ALU.add)
                last.then_inc(biased, 1)
                pool.wait_ge(biased, g.n + 1)
                pool.tensor_tensor(bias01[:, :, :], bias0[:, :, :], bias1[:, :, :], ALU.add).then_inc(bias_sum, 1)
                if not (isinstance(g.n, int) and g.n < 2):
                    pool.wait_ge(part_done, g.n - 1)
                pool.wait_ge(bias_sum, g.n + 1)
                pool.tensor_tensor(base[:, g.buf], bias01[:, :, :], x2[:, :, :], ALU.add).then_inc(base_done, 1)

            def before():
                pool.memset(ident[:, :], 0.0).then_inc(ident_zero, 1)
                pool.memset(minus_half[:, :], -0.5).then_inc(half_ready, 1)
                pool.wait_ge(ident_zero, 1)
                pool.affine_select(out=ident[:, :], in_=ident[:, :], compare_op=ALU.not_equal, fill=1.0, base=0,
                                   pattern=[[-1, P]], channel_multiplier=1).then_inc(ident_ready, 1)
                pool.wait_ge(half_ready, 1)
                first_norm(Group(0, 0))
                pool.wait_ge(wi_loaded, 16)
                for q in range(STEPS):
                    pool.wait_ge(wi_hi_ready, q + 1)
                    cols = slice(q * CS * P, (q + 1) * CS * P)
                    pool.tensor_tensor(wi_lo[:, :, cols], wi[:, :, cols], wi_hi[:, :, cols].bitcast(F32),
                                       ALU.subtract).then_inc(wi_lo_ready, 1)
                    if q == 0:
                        second_norm(Group(0, 0))
                    if q == 1:
                        first_norm(Group(0, 1))
                pool.wait_ge(rows_loaded, 32)
                residual(Group(0, 0))
                pool.wait_ge(wo_loaded, 16)
                for q in range(STEPS):
                    pool.wait_ge(wo_hi_ready, q + 1)
                    chunk = slice(q * CS, (q + 1) * CS)
                    pool.tensor_tensor(wo_lo[:, chunk], wo[:, chunk], wo_hi[:, chunk].bitcast(F32),
                                       ALU.subtract).then_inc(wo_lo_ready, 1)

            def body(g, first=False, left=2):
                if left == 2:
                    first_norm(g + 2)
                if left >= 1:
                    second_norm(g + 1)
                    residual(g + 1)

            run(pool, before, body)

        @block.scalar
        def _(act):
            def keep_xn_t(g):
                act.wait_ge(xn_turned, g.n + 1)
                act.copy(xn_t[:, :, :, :], ps_turn[:, :]).then_inc(xn_t_done, 1)

            def exps(g):
                act.wait_ge(centred_done, g.n + 1)
                act.activation(probs[:, :, :], centred[:, :, :], ACT.Exp, scale=float(D) ** -0.5
                               ).then_inc(probs_done, 1)

            def keep_probs_t(g):
                act.wait_ge(probs_turned, g.n + 1)
                act.copy(probs_t[:, :], ps_turn[:, 0:P]).then_inc(probs_t_done, 1)

            def keep_x2t(g):
                act.wait_ge(x2_turned, g.n + 1)
                act.copy(x2t_hi[:, g.buf].rearrange("p k (t n) -> p t k n", t=TILES),
                         ps_turn2[:, :].rearrange("p (t k n) -> p t k n", t=TILES, k=KC)
                         ).then_inc(x2t_hi_done, 1)

            def hidden(g, q):
                n = g.n * STEPS + q
                if not (isinstance(g.n, int) and n < 2):
                    act.wait_ge(hid_lo_done, n - 1)
                act.wait_ge(hid_ready, n + 1)
                for c in range(CS):
                    chunk = q * CS + c
                    last = act.activation(hid[:, q % 2, c], ps_hid[q % 2][:, c * GROUP:(c + 1) * GROUP],
                                          ACT.Gelu if chunk < FC // E else ACT.Relu,
                                          bias=b_in_sb[:, chunk:chunk + 1])
                last.then_inc(hid_taken, 1)
                act.wait_ge(hid_taken, n + 1)
                act.copy(hid_hi[:, q], hid[:, q % 2]).then_inc(hid_hi_done, 1)

            def before():
                keep_xn_t(Group(0, 0))
                act.wait_ge(wi_loaded, 16)
                for q in range(STEPS):
                    cols = slice(q * CS * P, (q + 1) * CS * P)
                    act.copy(wi_hi[:, :, cols], wi[:, :, cols]).then_inc(wi_hi_ready, 1)
                    if q == 0:
                        exps(Group(0, 0))
                        keep_probs_t(Group(0, 0))
                keep_x2t(Group(0, 0))
                keep_xn_t(Group(0, 1))
                act.wait_ge(wo_loaded, 16)
                for q in range(STEPS):
                    chunk = slice(q * CS, (q + 1) * CS)
                    act.copy(wo_hi[:, chunk], wo[:, chunk]).then_inc(wo_hi_ready, 1)
                exps(Group(0, 1))
                keep_probs_t(Group(0, 1))
                act.wait_ge(b_in_loaded, 16)

            def body(g, first=False, left=2):
                hidden(g, 0)
                hidden(g, 1)
                if left == 2:
                    keep_xn_t(g + 2)
                hidden(g, 2)
                if left >= 1:
                    keep_x2t(g + 1)
                hidden(g, 3)
                if left == 2:
                    exps(g + 2)
                    keep_probs_t(g + 2)

            run(act, before, body)

        @block.vector
        def _(dve):
            def norm_stats(g, src, stats, mean_var, var_eps, stats_done, aggr_done, var_done):
                for t in range(TILES):
                    last = dve.bn_stats(stats[:, t], src[:, t])
                last.then_inc(stats_done, 1)
                dve.wait_ge(stats_done, g.n + 1)
                dve.sem_inc(dve_passed, 1)
                for t in range(TILES):
                    last = dve.bn_aggr(mean_var[:, t], stats[:, t])
                last.then_inc(aggr_done, 1)
                dve.wait_ge(aggr_done, g.n + 1)
                dve.tensor_scalar(var_eps[:, :], mean_var[:, :, 1], EPS, None, ALU.add).then_inc(var_done, 1)

            def norm(src, dst, mean_var, rstd, done):
                for t in range(TILES):
                    last = dve.tensor_scalar(dst[:, t], src[:, t], mean_var[:, t, 0:1], rstd[:, t:t + 1],
                                             ALU.subtract, ALU.mult)
                last.then_inc(done, 1)

            def first_stats(g):
                dve.wait_ge(x_loaded[g.buf], 16 * (g.turn + 1))
                norm_stats(g, x_sb[:, g.buf], stats, mean_var, var_eps, stats_done, aggr_done, var_done)

            def first_norm(g):
                if not (isinstance(g.n, int) and g.n == 0):
                    dve.wait_ge(xn_turned, g.n)
                dve.wait_ge(rstd_done, g.n + 1)
                norm(x_sb[:, g.buf], xn, mean_var, rstd, xn_done)

            def mask_scores(g):
                dve.wait_ge(scores_done, g.n + 1)
                dve.tensor_tensor(masked[:, :, :], ps_score[:, 0:TILES * S].rearrange("p (t m) -> p t m", t=TILES),
                                  penalty[:, bass.ts(g.n, TILES)], ALU.add).then_inc(masked_done, 1)
                dve.wait_ge(masked_done, g.n + 1)
                dve.tensor_reduce(row_max[:, :], masked[:, :, :], AX_X, ALU.max).then_inc(max_done, 1)
                dve.wait_ge(max_done, g.n + 1)
                dve.tensor_tensor(centred[:, :, :], masked[:, :, :],
                                  row_max[:, :].unsqueeze(2).to_broadcast([P, TILES, S]),
                                  ALU.subtract).then_inc(centred_done, 1)

            def sum_probs(g):
                dve.wait_ge(probs_done, g.n + 1)
                dve.tensor_reduce(row_sum[:, :], probs[:, :, :], AX_X, ALU.add).then_inc(sum_done, 1)
                dve.wait_ge(sum_done, g.n + 1)
                dve.reciprocal(row_inv[:, :], row_sum[:, :]).then_inc(inv_done, 1)
                dve.wait_ge(inv_done, g.n + 1)
                dve.scalar_tensor_tensor(out=row_scale[:, :], in0=row_max[:, :], scalar=0.1 * NEG,
                                         in1=row_inv[:, :], op0=ALU.is_gt, op1=ALU.mult).then_inc(scale_done, 1)

            def add_readout(g):
                dve.wait_ge(read_done, g.n + 1)
                if not (isinstance(g.n, int) and g.n == 0):
                    dve.wait_ge(base_done, g.n)
                dve.wait_ge(scale_done, g.n + 1)
                for t in range(TILES):
                    last = dve.scalar_tensor_tensor(out=x2[:, t], in0=ps_read[t][:, 0:D],
                                                    scalar=row_scale[:, t:t + 1], in1=x_sb[:, g.buf, t],
                                                    op0=ALU.mult, op1=ALU.add)
                last.then_inc(x2_done, 1)

            def second_stats(g):
                dve.wait_ge(x2_done, g.n + 1)
                norm_stats(g, x2, stats2, mean_var2, var_eps2, stats2_done, aggr2_done, var2_done)

            def second_norm(g):
                if not (isinstance(g.n, int) and g.n == 0):
                    dve.wait_ge(x2_turned, g.n)
                dve.wait_ge(rstd2_done, g.n + 1)
                norm(x2, x2n, mean_var2, rstd2, x2n_done)

            def gate(g):
                dve.wait_ge(x2n_done, g.n + 1)
                for t in range(TILES):
                    last = dve.tensor_tensor_reduce(gate_prod[:, t], x2n[:, t], gate_diff[:, :], 1.0, 0.0, ALU.mult,
                                                    ALU.add, gate_sum[:, t:t + 1])
                last.then_inc(gate_done, 1)
                dve.wait_ge(gate_done, g.n + 1)
                dve.tensor_scalar(chosen[:, g.buf, 0], gate_sum[:, :], 0.0, None, ALU.is_ge)
                dve.tensor_scalar(chosen[:, g.buf, 1], gate_sum[:, :], 0.0, None, ALU.is_lt).then_inc(chosen_done, 1)

            def x2t_low(g):
                dve.wait_ge(x2t_hi_done, g.n + 1)
                dve.tensor_tensor(x2t_lo[:, g.buf].rearrange("p k (t n) -> p t k n", t=TILES),
                                  ps_turn2[:, :].rearrange("p (t k n) -> p t k n", t=TILES, k=KC),
                                  x2t_hi[:, g.buf].bitcast(F32).rearrange("p k (t n) -> p t k n", t=TILES),
                                  ALU.subtract).then_inc(x2t_lo_done, 1)

            def hidden_low(g, q):
                n = g.n * STEPS + q
                if not (isinstance(g.n, int) and g.n == 0):
                    dve.wait_ge(second_done, n + 1 - STEPS)
                dve.wait_ge(hid_hi_done, n + 1)
                dve.tensor_tensor(hid_lo[:, q], hid[:, q % 2], hid_hi[:, q].bitcast(F32),
                                  ALU.subtract).then_inc(hid_lo_done, 1)

            def add_expert0(g):
                if not (isinstance(g.n, int) and g.n == 0):
                    dve.wait_ge(out_done, g.n)
                dve.wait_ge(base_done, g.n + 1)
                dve.wait_ge(second_done, g.n * STEPS + 2)
                for t in range(TILES):
                    last = dve.scalar_tensor_tensor(out=part[:, t], in0=ps_y[0][:, t * D:(t + 1) * D],
                                                    scalar=chosen[:, g.buf, 0, t:t + 1], in1=base[:, g.buf, t],
                                                    op0=ALU.mult, op1=ALU.add)
                last.then_inc(part_done, 1)

            def add_expert1(g):
                if not (isinstance(g.n, int) and g.n < 2):
                    dve.wait_ge(stored[g.buf], 16 * g.turn)
                dve.wait_ge(part_done, g.n + 1)
                dve.wait_ge(second_done, g.n * STEPS + 4)
                for t in range(TILES):
                    last = dve.scalar_tensor_tensor(out=out_sb[:, g.buf, t], in0=ps_y[1][:, t * D:(t + 1) * D],
                                                    scalar=chosen[:, g.buf, 1, t:t + 1], in1=part[:, t],
                                                    op0=ALU.mult, op1=ALU.add)
                last.then_inc(out_done, 1)

            def before():
                g0, g1 = Group(0, 0), Group(0, 1)
                first_stats(g0)
                first_norm(g0)
                dve.wait_ge(mask_loaded, 32)
                dve.tensor_scalar(penalty[:, :, :], mask_u8[:, :, :], -1.0, -NEG, ALU.add, ALU.mult
                                  ).then_inc(penalty_ready, 1)
                dve.wait_ge(penalty_ready, 1)
                mask_scores(g0)
                first_stats(g1)
                sum_probs(g0)
                add_readout(g0)
                second_stats(g0)
                second_norm(g0)
                dve.wait_ge(rows_loaded, 32)
                dve.tensor_tensor(gate_diff[:, :], gate_rows[:, 0], gate_rows[:, 1], ALU.subtract
                                  ).then_inc(gate_ready, 1)
                first_norm(g1)
                x2t_low(g0)
                dve.wait_ge(gate_ready, 1)
                gate(g0)
                mask_scores(g1)
                sum_probs(g1)

            def body(g, first=False, left=2):
                if left >= 1:
                    add_readout(g + 1)
                if left == 2:
                    first_stats(g + 2)
                hidden_low(g, 0)
                if left >= 1:
                    second_stats(g + 1)
                if left == 2:
                    first_norm(g + 2)
                hidden_low(g, 1)
                if not first:
                    add_expert1(g + -1)
                if left >= 1:
                    second_norm(g + 1)
                    gate(g + 1)
                hidden_low(g, 2)
                if left == 2:
                    mask_scores(g + 2)
                if left >= 1:
                    x2t_low(g + 1)
                hidden_low(g, 3)
                add_expert0(g)
                if left == 2:
                    sum_probs(g + 2)

            run(dve, before, body)
            add_expert1(Group(0, GROUPS - 1))

        @block.tensor
        def _(pe):
            def turn_xn(g):
                if not (isinstance(g.n, int) and g.n == 0):
                    pe.wait_ge(probs_t_done, g.n)
                pe.wait_ge(xn_done, g.n + 1)
                for t in range(TILES):
                    for k in range(KC):
                        last = pe.transpose(ps_turn[:, (t * KC + k) * P:(t * KC + k + 1) * P],
                                            xn[:, t, k * P:(k + 1) * P], ident[:, :])
                last.then_inc(xn_turned, 1)

            def scores(g):
                pe.wait_ge(xn_t_done, g.n + 1)
                if not (isinstance(g.n, int) and g.n == 0):
                    pe.wait_ge(masked_done, g.n)
                pe.wait_ge(ctx_t_loaded[g.buf], 16 * (g.turn + 1))
                for t in range(TILES):
                    for k in range(KC):
                        for h in range(2):
                            b = 2 * t + h
                            last = pe.matmul(ps_score[h * S:(h + 1) * S, t * S:(t + 1) * S],
                                             xn_t[:, t, k, h * S:(h + 1) * S],
                                             ctx_t_sb[:, g.buf, k, b * S:(b + 1) * S],
                                             start=(k == 0), stop=(k == KC - 1))
                last.then_inc(scores_done, 1)

            def turn_probs(g):
                pe.wait_ge(probs_done, g.n + 1)
                pe.transpose(ps_turn[:, 0:P], probs[:, :, :].rearrange("p t m -> p (t m)"), ident[:, :]
                             ).then_inc(probs_turned, 1)

            def readout(g):
                if not (isinstance(g.n, int) and g.n == 0):
                    pe.wait_ge(x2t_lo_done, g.n)
                pe.wait_ge(probs_t_done, g.n + 1)
                pe.wait_ge(ctx_loaded[g.buf], 16 * (g.turn + 1))
                pe.sem_inc(pe_passed, 1)
                for t in range(TILES):
                    for h in range(2):
                        last = pe.matmul(ps_read[t][h * S:(h + 1) * S, 0:D],
                                         probs_t[t * S:(t + 1) * S, h * S:(h + 1) * S],
                                         ctx_sb[t * S:(t + 1) * S, g.buf, h], start=True, stop=True)
                last.then_inc(read_done, 1)

            def turn_x2n(g):
                pe.wait_ge(x2n_done, g.n + 1)
                for t in range(TILES):
                    for k in range(KC):
                        last = pe.transpose(ps_turn2[:, (t * KC + k) * P:(t * KC + k + 1) * P],
                                            x2n[:, t, k * P:(k + 1) * P], ident[:, :])
                last.then_inc(x2_turned, 1)

            def first_product(g, q, first=False):
                n = g.n * STEPS + q
                if first:
                    pe.wait_ge(wi_lo_ready, q + 1)
                if not first or q >= 2:
                    pe.wait_ge(hid_taken, n - 1)
                if q == 0:
                    pe.wait_ge(x2t_lo_done, g.n + 1)
                for c in range(CS):
                    cols = slice((q * CS + c) * P, (q * CS + c + 1) * P)
                    dst = ps_hid[q % 2][:, c * GROUP:(c + 1) * GROUP]
                    for k in range(KC):
                        hi, lo = x2t_hi[:, g.buf, k], x2t_lo[:, g.buf, k]
                        pe.matmul(dst, wi_hi[:, k, cols], hi, start=(k == 0), stop=False)
                        pe.matmul(dst, wi_hi[:, k, cols], lo, start=False, stop=False)
                        last = pe.matmul(dst, wi_lo[:, k, cols], hi, start=False, stop=(k == KC - 1))
                last.then_inc(hid_ready, 1)

            def second_product(g, q, first=False):
                n = g.n * STEPS + q
                e = q * CS // (FC // E)
                if first:
                    pe.wait_ge(wo_lo_ready, (1, STEPS)[q])
                elif q == 0:
                    pe.wait_ge(part_done, g.n)
                elif q == STEPS // 2:
                    pe.wait_ge(out_done, g.n)
                pe.wait_ge(hid_lo_done, n + 1)
                for c in range(CS):
                    chunk = q * CS + c
                    for t in range(TILES):
                        dst = ps_y[e][:, t * D:(t + 1) * D]
                        toks = slice(t * P, (t + 1) * P)
                        opens = chunk % (FC // E) == 0 and t == 0
                        closes = chunk % (FC // E) == FC // E - 1
                        pe.matmul(dst, hid_hi[:, q, c, toks], wo_hi[:, chunk], start=opens, stop=False,
                                  skip_group_check=True)
                        pe.matmul(dst, hid_hi[:, q, c, toks], wo_lo[:, chunk], start=False, stop=False,
                                  skip_group_check=True)
                        last = pe.matmul(dst, hid_lo[:, q, c, toks], wo_hi[:, chunk], start=False, stop=closes,
                                         skip_group_check=True)
                last.then_inc(second_done, 1)

            def before():
                pe.wait_ge(ident_ready, 1)
                g0, g1 = Group(0, 0), Group(0, 1)
                turn_xn(g0)
                scores(g0)
                turn_probs(g0)
                readout(g0)
                turn_x2n(g0)
                turn_xn(g1)
                scores(g1)
                turn_probs(g1)

            def body(g, first=False, left=2):
                first_product(g, 0, first)
                if not first:
                    second_product(g + -1, 2)
                if left >= 1:
                    readout(g + 1)
                first_product(g, 1, first)
                if not first:
                    second_product(g + -1, 3)
                if left == 2:
                    turn_xn(g + 2)
                first_product(g, 2, first)
                second_product(g, 0, first)
                if left == 2:
                    scores(g + 2)
                if left >= 1:
                    turn_x2n(g + 1)
                first_product(g, 3, first)
                second_product(g, 1, first)
                if left == 2:
                    turn_probs(g + 2)

            run(pe, before, body)
            second_product(Group(0, GROUPS - 1), 2)
            second_product(Group(0, GROUPS - 1), 3)


def kernel(x, ctx_2048, mask_BxS2_bk0, L0_ffn_Wg, L0_ffn_W0a, L0_ffn_b0a, L0_ffn_W0b, L0_ffn_b0b,
           L0_ffn_W1a, L0_ffn_b1a, L0_ffn_W1b, L0_ffn_b1b):
    import numpy as np
    import concourse.bacc as bacc
    from concourse.bass_utils import run_bass_kernel_spmd

    ctx_np = np.asarray(ctx_2048)
    ctx_t = ctx_np.reshape(GROUPS, 4, S, KC, P).transpose(0, 4, 3, 1, 2).reshape(GROUPS, P, KC, 4 * S)
    ctx = ctx_np.reshape(GROUPS, TILES, 2, S, D).transpose(0, 1, 3, 2, 4).reshape(GROUPS, P, 2, D)
    mask = np.asarray(mask_BxS2_bk0).reshape(B // 2, 2, S).transpose(1, 0, 2)
    w_in = np.concatenate([np.asarray(L0_ffn_W0a), np.asarray(L0_ffn_W1a)]).reshape(E * F, KC, P).transpose(2, 1, 0)
    b_in = np.concatenate([np.asarray(L0_ffn_b0a), np.asarray(L0_ffn_b1a)]).reshape(FC, P).T
    w_out = np.concatenate([np.asarray(L0_ffn_W0b).T, np.asarray(L0_ffn_W1b).T]).reshape(FC, P, D).transpose(1, 0, 2)
    b_out = np.stack([np.asarray(L0_ffn_b0b), np.asarray(L0_ffn_b1b)])[None]
    gate_w = np.asarray(L0_ffn_Wg)[None]
    arrays = {
        "x": np.asarray(x).reshape(B * S, D), "ctx": ctx, "ctx_t": ctx_t, "mask": mask, "gate_w": gate_w,
        "w_in": w_in, "b_in": b_in, "w_out": w_out, "b_out": b_out,
    }
    arrays = {name: np.ascontiguousarray(a) for name, a in arrays.items()}

    nc = bacc.Bacc("TRN2", target_bir_lowering=False, num_devices=1)
    aps = {name: nc.dram_tensor(name, a.shape, mybir.dt.from_np(a.dtype), kind="ExternalInput").ap()
           for name, a in arrays.items()}
    aps["out"] = nc.dram_tensor("out", (B * S, D), F32, kind="ExternalOutput").ap()
    xattn_ffn(nc, **aps)
    result = run_bass_kernel_spmd(nc, [arrays], core_ids=[0])
    return result.results[0]["out"].reshape(B, S, D)
```

```python
from contextlib import ExitStack

import concourse.bass as bass
from concourse import mybir

P = 128
B, S, D = 32, 64, 256
F = 512
E = 2
TILES = 2
GROUP = TILES * P
GROUPS = B * S // GROUP
KC = D // P
FC = E * F // P
CS = 2
STEPS = FC // CS
LAG = 2
WARM = [44, 8, 18, 6, 8, 20, 8]
NEG = -1e30
EPS = 1e-5

ALU = mybir.AluOpType
ACT = mybir.ActivationFunctionType
F32 = mybir.dt.float32
F32R = mybir.dt.float32r
BF16 = mybir.dt.bfloat16
U8 = mybir.dt.uint8
AX_X = mybir.AxisListType.X


class Group:

    def __init__(self, pair, offset):
        self.pair, self.offset = pair, offset
        self.n = pair * 2 + offset
        self.buf = offset % 2
        self.turn = pair + offset // 2

    def __add__(self, k):
        return Group(self.pair, self.offset + k)


def xattn_ffn(nc, x, ctx, ctx_t, mask, gate_w, w_in, b_in, w_out, b_out, out):
    x_tok = x.rearrange("(g t p) d -> g p t d", t=TILES, p=P)
    out_tok = out.rearrange("(g t p) d -> g p t d", t=TILES, p=P)

    with ExitStack() as stack:
        def sb(name, shape, dt=F32):
            return stack.enter_context(nc.sbuf_tensor(name, shape, dt))

        def bank(name):
            return stack.enter_context(nc.psum_tensor(name, [P, 512], F32))

        def sem(name):
            return stack.enter_context(nc.semaphore(name))

        ident = sb("ident", [P, P])
        zeros = sb("zeros", [P, P], BF16)
        minus_half = sb("minus_half", [P, TILES])
        minus_one = sb("minus_one", [P, TILES])
        eps = sb("eps", [P, TILES])
        unused = sb("unused", [P, TILES])
        mask_u8 = sb("mask_u8", [P, B // 2, S], U8)
        penalty = sb("penalty", [P, B // 2, S])
        gate_rows = sb("gate_rows", [P, E, D])
        gate_diff = sb("gate_diff", [P, D])
        b_in_sb = sb("b_in_sb", [P, FC])
        b_out_sb = sb("b_out_sb", [P, E, D])
        wi = sb("wi", [P, KC, E * F])
        wi_hi = sb("wi_hi", [P, KC, E * F], F32R)
        wi_lo = sb("wi_lo", [P, KC, E * F], F32R)
        wo = sb("wo", [P, FC, D])
        wo_hi = sb("wo_hi", [P, FC, D], F32R)
        wo_lo = sb("wo_lo", [P, FC, D], F32R)
        x_sb = sb("x_sb", [P, 2, TILES, D])
        ctx_t_sb = sb("ctx_t_sb", [P, 2, KC, 4 * S])
        ctx_sb = sb("ctx_sb", [P, 2, 2, D])
        stats = sb("stats", [P, TILES, 6])
        mean_var = sb("mean_var", [P, TILES, 2])
        var_eps = sb("var_eps", [P, TILES])
        minus_mean = sb("minus_mean", [P, TILES])
        rstd = sb("rstd", [P, TILES])
        xn = sb("xn", [P, TILES, D])
        xn_t = sb("xn_t", [P, TILES, KC, P])
        masked = sb("masked", [P, TILES, S])
        row_max = sb("row_max", [P, TILES])
        centred = sb("centred", [P, TILES, S])
        probs = sb("probs", [P, TILES, S])
        probs_t = sb("probs_t", [P, P])
        row_sum = sb("row_sum", [P, TILES])
        row_inv = sb("row_inv", [P, TILES])
        row_scale = sb("row_scale", [P, TILES])
        x2 = sb("x2", [P, 2, TILES, D])
        stats2 = sb("stats2", [P, TILES, 6])
        mean_var2 = sb("mean_var2", [P, TILES, 2])
        var_eps2 = sb("var_eps2", [P, TILES])
        minus_mean2 = sb("minus_mean2", [P, TILES])
        rstd2 = sb("rstd2", [P, TILES])
        x2n = sb("x2n", [P, 2, TILES, D])
        x2t_hi = sb("x2t_hi", [P, 2, KC, GROUP], F32R)
        x2t_lo = sb("x2t_lo", [P, 2, KC, GROUP], F32R)
        gate_prod = sb("gate_prod", [P, TILES, D])
        gate_sum = sb("gate_sum", [P, TILES])
        chosen = sb("chosen", [P, 2, E, TILES])
        bias0 = sb("bias0", [P, TILES, D])
        bias1 = sb("bias1", [P, TILES, D])
        bias01 = sb("bias01", [P, TILES, D])
        base = sb("base", [P, 2, TILES, D])
        hid = sb("hid", [P, 2, CS, GROUP])
        hid_hi = sb("hid_hi", [P, STEPS, CS, GROUP], F32R)
        hid_lo = sb("hid_lo", [P, STEPS, CS, GROUP], F32R)
        part = sb("part", [P, TILES, D])
        out_sb = sb("out_sb", [P, 2, TILES, D])

        ps_hid = [bank(f"ps_hid{i}") for i in range(2)]
        ps_y = [bank(f"ps_y{e}") for e in range(E)]
        ps_read = [bank(f"ps_read{j}") for j in range(2)]
        ps_turn = bank("ps_turn")
        ps_score = bank("ps_score")

        x0_loaded = sem("x0_loaded")
        x_loaded = [sem(f"x_loaded{i}") for i in range(2)]
        ctx_t_loaded = [sem(f"ctx_t_loaded{i}") for i in range(2)]
        ctx_loaded = [sem(f"ctx_loaded{i}") for i in range(2)]
        stored = [sem(f"stored{i}") for i in range(2)]
        mask_loaded = sem("mask_loaded")
        rows_loaded = sem("rows_loaded")
        b_in_loaded = sem("b_in_loaded")
        wi_loaded = sem("wi_loaded")
        wo_loaded = [sem(f"wo_loaded{e}") for e in range(E)]
        ident_zero = sem("ident_zero")
        ident_ready = sem("ident_ready")
        zeros_ready = sem("zeros_ready")
        consts_ready = sem("consts_ready")
        penalty_ready = sem("penalty_ready")
        gate_ready = sem("gate_ready")
        wi_hi_ready = sem("wi_hi_ready")
        wi_lo_ready = sem("wi_lo_ready")
        wi_lo2_ready = sem("wi_lo2_ready")
        wo_hi_ready = sem("wo_hi_ready")
        wo_lo_ready = sem("wo_lo_ready")
        wo_lo1_ready = sem("wo_lo1_ready")
        dve_passed, pe_passed, pool_passed = sem("dve_passed"), sem("pe_passed"), sem("pool_passed")
        xn_done = sem("xn_done")
        read_done = sem("read_done")
        x2n_done = sem("x2n_done")
        x2_turned = sem("x2_turned")
        stats_done = sem("stats_done")
        aggr_done = sem("aggr_done")
        var_done = sem("var_done")
        rstd_done = sem("rstd_done")
        xn_turned = sem("xn_turned")
        xn_t_done = sem("xn_t_done")
        scores_done = sem("scores_done")
        masked_done = sem("masked_done")
        max_done = sem("max_done")
        centred_done = sem("centred_done")
        probs_done = sem("probs_done")
        probs_turned = sem("probs_turned")
        probs_t_done = sem("probs_t_done")
        sum_done = sem("sum_done")
        inv_done = sem("inv_done")
        scale_done = sem("scale_done")
        x2_done = sem("x2_done")
        stats2_done = sem("stats2_done")
        aggr2_done = sem("aggr2_done")
        var2_done = sem("var2_done")
        rstd2_done = sem("rstd2_done")
        x2t_hi_done = sem("x2t_hi_done")
        x2t_lo_done = sem("x2t_lo_done")
        gate_done = sem("gate_done")
        chosen_done = sem("chosen_done")
        biased = sem("biased")
        bias_sum = sem("bias_sum")
        base_done = sem("base_done")
        part_done = sem("part_done")
        out_done = sem("out_done")
        hid_ready = sem("hid_ready")
        hid_taken = sem("hid_taken")
        hid_hi_done = sem("hid_hi_done")
        hid_lo_done = sem("hid_lo_done")
        second_done = sem("second_done")

        block = stack.enter_context(nc.Block())

        def run(engine, before, body):
            before()
            body(Group(0, 0), first=True)
            with engine.Fori(0, (GROUPS - 4) // 2) as pair:
                body(Group(pair, 1))
                body(Group(pair, 2))
            body(Group(0, GROUPS - 3), left=2)
            body(Group(0, GROUPS - 2), left=1)
            body(Group(0, GROUPS - 1), left=0)

        @block.sync
        def _(sp):
            def load_x(g, again=True):
                if again:
                    sp.wait_ge(x2_done, g.n - 1)
                sp.dma_start(x_sb[:, g.buf], x_tok[g.n]).then_inc(x_loaded[g.buf], 16)

            def load_ctx_t(g, again=True):
                if again:
                    sp.wait_ge(scores_done, g.n - 1)
                sp.dma_start(ctx_t_sb[:, g.buf], ctx_t[g.n]).then_inc(ctx_t_loaded[g.buf], 16)

            def load_ctx(g, again=True):
                if again:
                    sp.wait_ge(read_done, (g.n - 1) * TILES)
                sp.dma_start(ctx_sb[:, g.buf], ctx[g.n]).then_inc(ctx_loaded[g.buf], 16)

            def before():
                g0, g1 = Group(0, 0), Group(0, 1)
                sp.dma_start(x_sb[:, 0, 0], x_tok[0, :, 0]).then_inc(x0_loaded, 16)
                sp.dma_start(x_sb[:, 0, 1], x_tok[0, :, 1]).then_inc(x_loaded[0], 16)
                for i in range(2):
                    sp.sem_inc(stored[i], 16)
                for h in range(2):
                    sp.dma_start(mask_u8[h * S:(h + 1) * S], mask[h:h + 1].to_broadcast([S, B // 2, S])
                                 ).then_inc(mask_loaded, 16)
                load_ctx_t(g0, False)
                load_ctx(g0, False)
                load_x(g1, False)
                sp.dma_start(wi[:, :, :], w_in).then_inc(wi_loaded, 16)
                sp.dma_start(gate_rows[:, :, :], gate_w.to_broadcast([P, E, D])).then_inc(rows_loaded, 16)
                sp.dma_start(b_out_sb[:, :, :], b_out.to_broadcast([P, E, D])).then_inc(rows_loaded, 16)
                sp.dma_start(b_in_sb[:, :], b_in).then_inc(b_in_loaded, 16)
                load_ctx_t(g1, False)
                for e in (1, 0):
                    chunks = slice(e * FC // E, (e + 1) * FC // E)
                    sp.dma_start(wo[:, chunks], w_out[:, chunks]).then_inc(wo_loaded[e], 16)
                load_ctx(g1, False)
                load_x(Group(0, 2))

            def store(g):
                sp.wait_ge(out_done, g.n + 1)
                sp.dma_start(out_tok[g.n], out_sb[:, g.buf]).then_inc(stored[g.buf], 16)

            def body(g, first=False, left=3):
                if left >= 2:
                    load_ctx_t(g + 2)
                    load_ctx(g + 2)
                if left >= 3:
                    load_x(g + 3)
                if not first:
                    store(g + -1)

            run(sp, before, body)
            store(Group(0, GROUPS - 1))
            for i in range(2):
                sp.wait_ge(stored[i], 16 * (GROUPS // 2 + 1))

        @block.gpsimd
        def _(pool):
            def norm(g, src, dst, mean_var, var_eps, minus_mean, rstd, aggr_done, var_done, rstd_done, done):
                pool.wait_ge(aggr_done, g.n + 1)
                pool.tensor_tensor(var_eps[:, :], mean_var[:, :, 1], eps[:, :], ALU.add).then_inc(var_done, 1)
                pool.tensor_tensor(minus_mean[:, :], mean_var[:, :, 0], minus_one[:, :], ALU.mult)
                pool.wait_ge(var_done, g.n + 1)
                pool.tensor_tensor(rstd[:, :], var_eps[:, :], minus_half[:, :], ALU.pow).then_inc(rstd_done, 1)
                pool.wait_ge(rstd_done, g.n + 1)
                pool.sem_inc(pool_passed, 1)
                for t in range(TILES):
                    pool.tensor_scalar(dst[:, t], src[:, t], minus_mean[:, t:t + 1], rstd[:, t:t + 1],
                                       ALU.add, ALU.mult).then_inc(done, 1)

            def first_norm(g):
                if not (isinstance(g.n, int) and g.n == 0):
                    pool.wait_ge(xn_turned, g.n)
                norm(g, x_sb[:, g.buf], xn, mean_var, var_eps, minus_mean, rstd, aggr_done, var_done, rstd_done,
                     xn_done)

            def second_norm(g):
                if not (isinstance(g.n, int) and g.n < 2):
                    pool.wait_ge(x2_turned, (g.n - 1) * TILES)
                    pool.wait_ge(gate_done, g.n - 1)
                norm(g, x2[:, g.buf], x2n[:, g.buf], mean_var2, var_eps2, minus_mean2, rstd2, aggr2_done, var2_done, rstd2_done,
                     x2n_done)

            def choose_bias(g):
                pool.wait_ge(chosen_done, g.n + 1)
                pool.sem_inc(pool_passed, 1)
                for t in range(TILES):
                    pool.tensor_scalar(bias0[:, t], b_out_sb[:, 0], chosen[:, g.buf, 0, t:t + 1], 0.0,
                                       ALU.mult, ALU.add)
                    last = pool.tensor_scalar(bias1[:, t], b_out_sb[:, 1], chosen[:, g.buf, 1, t:t + 1], 0.0,
                                              ALU.mult, ALU.add)
                last.then_inc(biased, 1)

            def residual(g):
                pool.wait_ge(biased, g.n + 1)
                pool.tensor_tensor(bias01[:, :, :], bias0[:, :, :], bias1[:, :, :], ALU.add).then_inc(bias_sum, 1)
                pool.wait_ge(bias_sum, g.n + 1)
                pool.tensor_tensor(base[:, g.buf], bias01[:, :, :], x2[:, g.buf], ALU.add).then_inc(base_done, 1)

            def before():
                pool.memset(ident[:, :], 0.0).then_inc(ident_zero, 1)
                for const, value in ((minus_half, -0.5), (minus_one, -1.0), (eps, EPS)):
                    pool.memset(const[:, :], value).then_inc(consts_ready, 1)
                pool.wait_ge(ident_zero, 1)
                pool.affine_select(out=ident[:, :], in_=ident[:, :], compare_op=ALU.not_equal, fill=1.0, base=0,
                                   pattern=[[-1, P]], channel_multiplier=1).then_inc(ident_ready, 1)
                pool.wait_ge(consts_ready, 3)
                pool.wait_ge(var_done, 1)
                pool.tensor_tensor(rstd[:, :], var_eps[:, :], minus_half[:, :], ALU.pow).then_inc(rstd_done, 1)
                first_norm(Group(0, 1))
                pool.wait_ge(var2_done, 1)
                pool.tensor_tensor(rstd2[:, :], var_eps2[:, :], minus_half[:, :], ALU.pow).then_inc(rstd2_done, 1)

                def out_lo(q, nth):
                    pool.wait_ge(wo_hi_ready, nth)
                    chunk = slice(q * CS, (q + 1) * CS)
                    pool.tensor_tensor(wo_lo[:, chunk], wo[:, chunk], wo_hi[:, chunk].bitcast(F32),
                                       ALU.subtract).then_inc(wo_lo_ready, 1)

                out_lo(2, 1)
                pool.wait_ge(wi_hi_ready, 3)
                cols = slice(2 * CS * P, 3 * CS * P)
                pool.tensor_tensor(wi_lo[:, :, cols], wi[:, :, cols], wi_hi[:, :, cols].bitcast(F32),
                                   ALU.subtract).then_inc(wi_lo2_ready, 1)
                first_norm(Group(0, 2))
                out_lo(0, 3)
                second_norm(Group(0, 1))
                out_lo(3, 2)
                pool.wait_ge(rows_loaded, 32)

            def body(g, first=False, left=3):
                if left >= 2 and not first:
                    first_norm(g + 2)
                choose_bias(g)
                if left >= 1 and not first:
                    second_norm(g + 1)
                residual(g)

            run(pool, before, body)

        @block.scalar
        def _(act):
            def keep_xn_t(g):
                act.wait_ge(xn_turned, g.n + 1)
                act.copy(xn_t[:, :, :, :], ps_turn[:, :]).then_inc(xn_t_done, 1)

            def exps(g):
                act.wait_ge(centred_done, g.n + 1)
                act.activation(probs[:, :, :], centred[:, :, :], ACT.Exp, scale=float(D) ** -0.5
                               ).then_inc(probs_done, 1)

            def keep_probs_t(g):
                act.wait_ge(probs_turned, g.n + 1)
                act.copy(probs_t[:, :], ps_turn[:, 0:P]).then_inc(probs_t_done, 1)

            def keep_x2t(g):
                for t in range(TILES):
                    act.wait_ge(x2_turned, g.n * TILES + t + 1)
                    last = act.copy(x2t_hi[:, g.buf, :, t * P:(t + 1) * P],
                                    ps_read[t][:, 0:D].rearrange("p (k n) -> p k n", k=KC))
                last.then_inc(x2t_hi_done, 1)

            def hidden(g, q):
                n = g.n * STEPS + q
                if not (isinstance(g.n, int) and n < 2):
                    act.wait_ge(hid_lo_done, n - 1)
                act.wait_ge(hid_ready, n + 1)
                for c in range(CS):
                    chunk = q * CS + c
                    last = act.activation(hid[:, q % 2, c], ps_hid[q % 2][:, c * GROUP:(c + 1) * GROUP],
                                          ACT.Gelu if chunk < FC // E else ACT.Relu,
                                          bias=b_in_sb[:, chunk:chunk + 1])
                last.then_inc(hid_taken, 1)
                act.wait_ge(hid_taken, n + 1)
                act.copy(hid_hi[:, q], hid[:, q % 2]).then_inc(hid_hi_done, 1)

            def out_hi(q):
                chunk = slice(q * CS, (q + 1) * CS)
                act.copy(wo_hi[:, chunk], wo[:, chunk]).then_inc(wo_hi_ready, 1)

            def before():
                g0, g1 = Group(0, 0), Group(0, 1)

                def in_hi(q):
                    cols = slice(q * CS * P, (q + 1) * CS * P)
                    act.copy(wi_hi[:, :, cols], wi[:, :, cols]).then_inc(wi_hi_ready, 1)

                keep_xn_t(g0)
                exps(g0)
                keep_probs_t(g0)
                act.wait_ge(wi_loaded, 16)
                in_hi(0)
                in_hi(1)
                keep_xn_t(g1)
                in_hi(2)
                in_hi(3)
                act.wait_ge(wo_loaded[1], 16)
                out_hi(2)
                out_hi(3)
                keep_x2t(g0)
                exps(g1)
                act.wait_ge(b_in_loaded, 16)
                act.wait_ge(consts_ready, 3)
                act.activation(unused[:, :], minus_one[:, :], ACT.Gelu)
                keep_probs_t(g1)
            def body(g, first=False, left=3):
                hidden(g, 0)
                if first:
                    act.wait_ge(wo_loaded[0], 16)
                    out_hi(0)
                hidden(g, 1)
                if first:
                    out_hi(1)
                if left >= 2:
                    keep_xn_t(g + 2)
                hidden(g, 2)
                if left >= 1:
                    keep_x2t(g + 1)
                if left >= 2:
                    exps(g + 2)
                hidden(g, 3)
                if left >= 2:
                    keep_probs_t(g + 2)

            run(act, before, body)

        @block.vector
        def _(dve):
            def norm_stats(g, src, stats, mean_var, stats_done, aggr_done, between=lambda: None):
                dve.bn_stats(stats[:, 0], src[:, 0])
                between()
                dve.bn_stats(stats[:, 1], src[:, 1]).then_inc(stats_done, 1)
                dve.wait_ge(stats_done, g.n + 1)
                if not isinstance(g.n, int):
                    dve.sem_inc(dve_passed, 1)
                for t in range(TILES):
                    last = dve.bn_aggr(mean_var[:, t], stats[:, t])
                last.then_inc(aggr_done, 1)

            def first_stats(g):
                if not (isinstance(g.n, int) and g.n == 0):
                    dve.wait_ge(xn_done, g.n * TILES)
                dve.wait_ge(x_loaded[g.buf], 16 * (g.turn + 1))
                norm_stats(g, x_sb[:, g.buf], stats, mean_var, stats_done, aggr_done)

            def mask_scores(g):
                dve.wait_ge(scores_done, g.n + 1)
                dve.tensor_tensor(masked[:, :, :], ps_score[:, 0:TILES * S].rearrange("p (t m) -> p t m", t=TILES),
                                  penalty[:, bass.ts(g.n, TILES)], ALU.add).then_inc(masked_done, 1)
                dve.wait_ge(masked_done, g.n + 1)
                dve.tensor_reduce(row_max[:, :], masked[:, :, :], AX_X, ALU.max).then_inc(max_done, 1)
                dve.wait_ge(max_done, g.n + 1)
                dve.tensor_tensor(centred[:, :, :], masked[:, :, :],
                                  row_max[:, :].unsqueeze(2).to_broadcast([P, TILES, S]),
                                  ALU.subtract).then_inc(centred_done, 1)

            def sum_probs(g):
                dve.wait_ge(probs_done, g.n + 1)
                dve.tensor_reduce(row_sum[:, :], probs[:, :, :], AX_X, ALU.add).then_inc(sum_done, 1)
                dve.wait_ge(sum_done, g.n + 1)
                dve.reciprocal(row_inv[:, :], row_sum[:, :]).then_inc(inv_done, 1)
                dve.wait_ge(inv_done, g.n + 1)
                dve.scalar_tensor_tensor(out=row_scale[:, :], in0=row_max[:, :], scalar=0.1 * NEG,
                                         in1=row_inv[:, :], op0=ALU.is_gt, op1=ALU.mult).then_inc(scale_done, 1)

            def add_readout(g):
                if not (isinstance(g.n, int) and g.n < 2):
                    dve.wait_ge(base_done, g.n - 1)
                dve.wait_ge(scale_done, g.n + 1)
                for t in range(TILES):
                    dve.wait_ge(read_done, g.n * TILES + t + 1)
                    last = dve.scalar_tensor_tensor(out=x2[:, g.buf, t], in0=ps_read[t][:, 0:D],
                                                    scalar=row_scale[:, t:t + 1], in1=x_sb[:, g.buf, t],
                                                    op0=ALU.mult, op1=ALU.add)
                last.then_inc(x2_done, 1)

            def second_stats(g):
                if not (isinstance(g.n, int) and g.n == 0):
                    dve.wait_ge(x2n_done, g.n * TILES)
                dve.wait_ge(x2_done, g.n + 1)
                norm_stats(g, x2[:, g.buf], stats2, mean_var2, stats2_done, aggr2_done)

            def gate(g):
                if not (isinstance(g.n, int) and g.n == 0):
                    dve.wait_ge(chosen_done, g.n)
                dve.wait_ge(x2n_done, (g.n + 1) * TILES)
                for t in range(TILES):
                    last = dve.tensor_tensor_reduce(gate_prod[:, t], x2n[:, g.buf, t], gate_diff[:, :], 1.0, 0.0, ALU.mult,
                                                    ALU.add, gate_sum[:, t:t + 1])
                last.then_inc(gate_done, 1)
                dve.wait_ge(gate_done, g.n + 1)
                dve.tensor_scalar(chosen[:, g.buf, 0], gate_sum[:, :], 0.0, None, ALU.is_ge)
                dve.tensor_scalar(chosen[:, g.buf, 1], gate_sum[:, :], 0.0, None, ALU.is_lt).then_inc(chosen_done, 1)

            def x2t_low(g):
                dve.wait_ge(x2t_hi_done, g.n + 1)
                for t in range(TILES):
                    toks = slice(t * P, (t + 1) * P)
                    last = dve.tensor_tensor(x2t_lo[:, g.buf, :, toks],
                                             ps_read[t][:, 0:D].rearrange("p (k n) -> p k n", k=KC),
                                             x2t_hi[:, g.buf, :, toks].bitcast(F32), ALU.subtract)
                last.then_inc(x2t_lo_done, 1)

            def hidden_low(g, q):
                n = g.n * STEPS + q
                if not (isinstance(g.n, int) and g.n == 0):
                    dve.wait_ge(second_done, n + 1 - STEPS)
                dve.wait_ge(hid_hi_done, n + 1)
                dve.tensor_tensor(hid_lo[:, q], hid[:, q % 2], hid_hi[:, q].bitcast(F32),
                                  ALU.subtract).then_inc(hid_lo_done, 1)

            def add_expert0(g):
                if not (isinstance(g.n, int) and g.n == 0):
                    dve.wait_ge(out_done, g.n)
                dve.wait_ge(base_done, g.n + 1)
                dve.wait_ge(second_done, g.n * STEPS + 2)
                for t in range(TILES):
                    last = dve.scalar_tensor_tensor(out=part[:, t], in0=ps_y[0][:, t * D:(t + 1) * D],
                                                    scalar=chosen[:, g.buf, 0, t:t + 1], in1=base[:, g.buf, t],
                                                    op0=ALU.mult, op1=ALU.add)
                last.then_inc(part_done, 1)

            def add_expert1(g):
                dve.wait_ge(stored[g.buf], 16 * (g.turn + 1))
                dve.wait_ge(part_done, g.n + 1)
                dve.wait_ge(second_done, g.n * STEPS + 4)
                for t in range(TILES):
                    last = dve.scalar_tensor_tensor(out=out_sb[:, g.buf, t], in0=ps_y[1][:, t * D:(t + 1) * D],
                                                    scalar=chosen[:, g.buf, 1, t:t + 1], in1=part[:, t],
                                                    op0=ALU.mult, op1=ALU.add)
                last.then_inc(out_done, 1)

            def in_lo(q):
                dve.wait_ge(wi_hi_ready, q + 1)
                cols = slice(q * CS * P, (q + 1) * CS * P)
                dve.tensor_tensor(wi_lo[:, :, cols], wi[:, :, cols], wi_hi[:, :, cols].bitcast(F32),
                                  ALU.subtract).then_inc(wi_lo_ready, 1)

            def out_lo_1():
                dve.wait_ge(wo_hi_ready, STEPS)
                chunk = slice(CS, 2 * CS)
                dve.tensor_tensor(wo_lo[:, chunk], wo[:, chunk], wo_hi[:, chunk].bitcast(F32),
                                  ALU.subtract).then_inc(wo_lo1_ready, 1)

            def before():
                g0, g1 = Group(0, 0), Group(0, 1)

                def norm_0(src, dst, mean_var, var_eps, rstd, aggr_done, var_done, rstd_done, done, beside=lambda: None):
                    dve.wait_ge(aggr_done, 1)
                    dve.tensor_scalar(var_eps[:, :], mean_var[:, :, 1], EPS, None, ALU.add).then_inc(var_done, 1)
                    beside()
                    dve.wait_ge(rstd_done, 1)
                    for t in range(TILES):
                        dve.tensor_scalar(dst[:, t], src[:, t], mean_var[:, t, 0:1], rstd[:, t:t + 1],
                                          ALU.subtract, ALU.mult).then_inc(done, 1)

                dve.memset(zeros[:, :], 0.0).then_inc(zeros_ready, 1)
                dve.wait_ge(x0_loaded, 16)
                norm_stats(g0, x_sb[:, 0], stats, mean_var, stats_done, aggr_done,
                           between=lambda: dve.wait_ge(x_loaded[0], 16))
                norm_0(x_sb[:, 0], xn, mean_var, var_eps, rstd, aggr_done, var_done, rstd_done, xn_done)
                dve.wait_ge(mask_loaded, 32)
                dve.tensor_scalar(penalty[:, :, :], mask_u8[:, :, :], -1.0, -NEG, ALU.add, ALU.mult
                                  ).then_inc(penalty_ready, 1)
                first_stats(g1)
                dve.wait_ge(penalty_ready, 1)
                mask_scores(g0)
                sum_probs(g0)
                add_readout(g0)
                second_stats(g0)
                norm_0(x2[:, 0], x2n[:, 0], mean_var2, var_eps2, rstd2, aggr2_done, var2_done, rstd2_done, x2n_done,
                       lambda: in_lo(0))
                mask_scores(g1)
                x2t_low(g0)
                first_stats(Group(0, 2))
                in_lo(1)
                sum_probs(g1)
                dve.wait_ge(rows_loaded, 32)
                dve.tensor_tensor(gate_diff[:, :], gate_rows[:, 0], gate_rows[:, 1], ALU.subtract
                                  ).then_inc(gate_ready, 1)
                add_readout(g1)
                second_stats(g1)

            def body(g, first=False, left=3):
                if not first:
                    hidden_low(g + -1, 3)
                if left >= 1 and not first:
                    sum_probs(g + 1)
                if not first:
                    add_expert0(g + -1)
                hidden_low(g, 0)
                if first:
                    dve.wait_ge(gate_ready, 1)
                    gate(g)
                    in_lo(3)
                elif left >= 1:
                    add_readout(g + 1)
                    second_stats(g + 1)
                hidden_low(g, 1)
                if first:
                    out_lo_1()
                if not first:
                    add_expert1(g + -1)
                hidden_low(g, 2)
                if left >= 2:
                    mask_scores(g + 2)
                if left >= 1:
                    x2t_low(g + 1)
                    gate(g + 1)
                if left >= 3:
                    first_stats(g + 3)

            run(dve, before, body)
            hidden_low(Group(0, GROUPS - 1), 3)
            add_expert0(Group(0, GROUPS - 1))
            add_expert1(Group(0, GROUPS - 1))

        @block.tensor
        def _(pe):
            def turn_xn(g):
                if not (isinstance(g.n, int) and g.n == 0):
                    pe.wait_ge(probs_t_done, g.n)
                for t in range(TILES):
                    pe.wait_ge(xn_done, g.n * TILES + t + 1)
                    for k in range(KC):
                        last = pe.transpose(ps_turn[:, (t * KC + k) * P:(t * KC + k + 1) * P],
                                            xn[:, t, k * P:(k + 1) * P], ident[:, :])
                last.then_inc(xn_turned, 1)

            def scores(g):
                pe.wait_ge(xn_t_done, g.n + 1)
                if not (isinstance(g.n, int) and g.n == 0):
                    pe.wait_ge(masked_done, g.n)
                pe.wait_ge(ctx_t_loaded[g.buf], 16 * (g.turn + 1))
                for t in range(TILES):
                    for k in range(KC):
                        for h in range(2):
                            b = 2 * t + h
                            last = pe.matmul(ps_score[h * S:(h + 1) * S, t * S:(t + 1) * S],
                                             xn_t[:, t, k, h * S:(h + 1) * S],
                                             ctx_t_sb[:, g.buf, k, b * S:(b + 1) * S],
                                             start=(k == 0), stop=(k == KC - 1))
                last.then_inc(scores_done, 1)

            def turn_probs(g):
                pe.wait_ge(probs_done, g.n + 1)
                pe.transpose(ps_turn[:, 0:P], probs[:, :, :].rearrange("p t m -> p (t m)"), ident[:, :]
                             ).then_inc(probs_turned, 1)

            def readout(g):
                if not (isinstance(g.n, int) and g.n == 0):
                    pe.wait_ge(x2t_lo_done, g.n)
                pe.wait_ge(probs_t_done, g.n + 1)
                pe.wait_ge(ctx_loaded[g.buf], 16 * (g.turn + 1))
                pe.sem_inc(pe_passed, 1)
                for t in range(TILES):
                    for h in range(2):
                        last = pe.matmul(ps_read[t][h * S:(h + 1) * S, 0:D],
                                         probs_t[t * S:(t + 1) * S, h * S:(h + 1) * S],
                                         ctx_sb[t * S:(t + 1) * S, g.buf, h], start=True, stop=True)
                    last.then_inc(read_done, 1)

            def turn_x2n(g):
                for t in range(TILES):
                    pe.wait_ge(x2n_done, g.n * TILES + t + 1)
                    for k in range(KC):
                        last = pe.transpose(ps_read[t][:, k * P:(k + 1) * P],
                                            x2n[:, g.buf, t, k * P:(k + 1) * P], ident[:, :])
                    last.then_inc(x2_turned, 1)

            def first_product(g, q, first=False, midway=lambda: None):
                n = g.n * STEPS + q
                if first:
                    if q == 2:
                        pe.wait_ge(wi_lo2_ready, 1)
                    else:
                        pe.wait_ge(wi_lo_ready, min(q + 1, 3))
                if not first or q >= 2:
                    pe.wait_ge(hid_taken, n - 1)
                if q == 0:
                    pe.wait_ge(x2t_hi_done, g.n + 1)
                def dst(c):
                    return ps_hid[q % 2][:, c * GROUP:(c + 1) * GROUP]

                def cols(c):
                    return slice((q * CS + c) * P, (q * CS + c + 1) * P)

                for c in range(CS):
                    for k in range(KC):
                        hi = x2t_hi[:, g.buf, k]
                        pe.matmul(dst(c), wi_hi[:, k, cols(c)], hi, start=(c == 0 and k == 0), stop=False,
                                  skip_group_check=True)
                        pe.matmul(dst(c), wi_lo[:, k, cols(c)], hi, start=False, stop=False, skip_group_check=True)
                midway()
                if q == 0:
                    pe.wait_ge(x2t_lo_done, g.n + 1)
                for c in range(CS):
                    for k in range(KC):
                        last = pe.matmul(dst(c), wi_hi[:, k, cols(c)], x2t_lo[:, g.buf, k], start=False,
                                         stop=(k == KC - 1), skip_group_check=True)
                last.then_inc(hid_ready, 1)

            def second_product(g, q, first=False):
                n = g.n * STEPS + q
                e = q * CS // (FC // E)
                if first:
                    if q == 0:
                        pe.wait_ge(wo_lo_ready, 2)
                    else:
                        pe.wait_ge(wo_lo_ready, 3)
                        pe.wait_ge(wo_lo1_ready, 1)
                elif q == 0:
                    pe.wait_ge(part_done, g.n)
                elif q == STEPS // 2:
                    pe.wait_ge(out_done, g.n)
                pe.wait_ge(hid_lo_done, n + 1)
                for c in range(CS):
                    chunk = q * CS + c
                    for t in range(TILES):
                        dst = ps_y[e][:, t * D:(t + 1) * D]
                        toks = slice(t * P, (t + 1) * P)
                        opens = chunk % (FC // E) == 0 and t == 0
                        closes = chunk % (FC // E) == FC // E - 1
                        pe.matmul(dst, hid_hi[:, q, c, toks], wo_hi[:, chunk], start=opens, stop=False,
                                  skip_group_check=True)
                        pe.matmul(dst, hid_hi[:, q, c, toks], wo_lo[:, chunk], start=False, stop=False,
                                  skip_group_check=True)
                        last = pe.matmul(dst, hid_lo[:, q, c, toks], wo_hi[:, chunk], start=False, stop=closes,
                                         skip_group_check=True)
                last.then_inc(second_done, 1)

            def before():
                g0, g1 = Group(0, 0), Group(0, 1)

                def keep_warm(count):
                    for _ in range(count):
                        pe.matmul(ps_y[1][:, 0:P], zeros[:, :], zeros[:, :], start=True, stop=True)

                pe.wait_ge(zeros_ready, 1)
                keep_warm(WARM[0])
                pe.wait_ge(ident_ready, 1)
                turn_xn(g0)
                keep_warm(WARM[1])
                scores(g0)
                keep_warm(WARM[2])
                turn_probs(g0)
                keep_warm(WARM[3])
                readout(g0)
                turn_xn(g1)
                keep_warm(WARM[4])
                scores(g1)
                keep_warm(WARM[5])
                turn_x2n(g0)
                keep_warm(WARM[6])

            def body(g, first=False, left=3):
                if first:
                    first_product(g, 0, first, midway=lambda: turn_probs(g + 1))
                else:
                    first_product(g, 0)
                    second_product(g + -1, 2)
                if left >= 1:
                    readout(g + 1)
                first_product(g, 1, first)
                if not first:
                    second_product(g + -1, 3)
                if left >= 2:
                    turn_xn(g + 2)
                first_product(g, 2, first)
                second_product(g, 0, first)
                if left >= 2:
                    scores(g + 2)
                if left >= 2:
                    turn_x2n(g + 1)
                first_product(g, 3, first)
                if left == 1:
                    turn_x2n(g + 1)
                second_product(g, 1, first)
                if left >= 2:
                    turn_probs(g + 2)

            run(pe, before, body)
            second_product(Group(0, GROUPS - 1), 2)
            second_product(Group(0, GROUPS - 1), 3)


def kernel(x, ctx_2048, mask_BxS2_bk0, L0_ffn_Wg, L0_ffn_W0a, L0_ffn_b0a, L0_ffn_W0b, L0_ffn_b0b,
           L0_ffn_W1a, L0_ffn_b1a, L0_ffn_W1b, L0_ffn_b1b):
    import numpy as np
    import concourse.bacc as bacc
    from concourse.bass_utils import run_bass_kernel_spmd

    ctx_np = np.asarray(ctx_2048)
    ctx_t = ctx_np.reshape(GROUPS, 4, S, KC, P).transpose(0, 4, 3, 1, 2).reshape(GROUPS, P, KC, 4 * S)
    ctx = ctx_np.reshape(GROUPS, TILES, 2, S, D).transpose(0, 1, 3, 2, 4).reshape(GROUPS, P, 2, D)
    mask = np.asarray(mask_BxS2_bk0).reshape(B // 2, 2, S).transpose(1, 0, 2)
    w_in = np.concatenate([np.asarray(L0_ffn_W0a), np.asarray(L0_ffn_W1a)]).reshape(E * F, KC, P).transpose(2, 1, 0)
    b_in = np.concatenate([np.asarray(L0_ffn_b0a), np.asarray(L0_ffn_b1a)]).reshape(FC, P).T
    w_out = np.concatenate([np.asarray(L0_ffn_W0b).T, np.asarray(L0_ffn_W1b).T]).reshape(FC, P, D).transpose(1, 0, 2)
    b_out = np.stack([np.asarray(L0_ffn_b0b), np.asarray(L0_ffn_b1b)])[None]
    gate_w = np.asarray(L0_ffn_Wg)[None]
    arrays = {
        "x": np.asarray(x).reshape(B * S, D), "ctx": ctx, "ctx_t": ctx_t, "mask": mask, "gate_w": gate_w,
        "w_in": w_in, "b_in": b_in, "w_out": w_out, "b_out": b_out,
    }
    arrays = {name: np.ascontiguousarray(a) for name, a in arrays.items()}

    nc = bacc.Bacc("TRN2", target_bir_lowering=False, num_devices=1)
    aps = {name: nc.dram_tensor(name, a.shape, mybir.dt.from_np(a.dtype), kind="ExternalInput").ap()
           for name, a in arrays.items()}
    aps["out"] = nc.dram_tensor("out", (B * S, D), F32, kind="ExternalOutput").ap()
    xattn_ffn(nc, **aps)
    result = run_bass_kernel_spmd(nc, [arrays], core_ids=[0])
    return result.results[0]["out"].reshape(B, S, D)
```

```python
from contextlib import ExitStack

import concourse.bass as bass
from concourse import mybir

P = 128
B, S, D = 32, 64, 256
F = 512
E = 2
TILES = 2
GROUP = TILES * P
GROUPS = B * S // GROUP
KC = D // P
FC = E * F // P
CS = 2
STEPS = FC // CS
NEG = -1e30
EPS = 1e-5

ALU = mybir.AluOpType
ACT = mybir.ActivationFunctionType
F32 = mybir.dt.float32
F32R = mybir.dt.float32r
BF16 = mybir.dt.bfloat16
U8 = mybir.dt.uint8
AX_X = mybir.AxisListType.X


class Group:

    def __init__(self, pair, offset):
        self.pair, self.offset = pair, offset
        self.n = pair * 2 + offset
        self.buf = offset % 2
        self.turn = pair + offset // 2

    def __add__(self, k):
        return Group(self.pair, self.offset + k)


def xattn_ffn(nc, x, ctx, ctx_t, mask, gate_w, w_in, b_in, w_out, b_out, out):
    x_tok = x.rearrange("(g t p) d -> g p t d", t=TILES, p=P)
    out_tok = out.rearrange("(g t p) d -> g p t d", t=TILES, p=P)

    with ExitStack() as stack:
        def sb(name, shape, dt=F32):
            return stack.enter_context(nc.sbuf_tensor(name, shape, dt))

        def bank(name):
            return stack.enter_context(nc.psum_tensor(name, [P, 512], F32))

        def sem(name):
            return stack.enter_context(nc.semaphore(name))

        ident = sb("ident", [P, P])
        zeros = sb("zeros", [P, P], BF16)
        minus_half = sb("minus_half", [P, TILES])
        minus_one = sb("minus_one", [P, TILES])
        eps = sb("eps", [P, TILES])
        unused = sb("unused", [P, TILES])
        mask_u8 = sb("mask_u8", [P, B // 2, S], U8)
        penalty = sb("penalty", [P, B // 2, S])
        gate_rows = sb("gate_rows", [P, E, D])
        gate_diff = sb("gate_diff", [P, D])
        b_in_sb = sb("b_in_sb", [P, FC])
        b_out_sb = sb("b_out_sb", [P, E, D])
        wi = sb("wi", [P, KC, E * F])
        wi_hi = sb("wi_hi", [P, KC, E * F], F32R)
        wi_lo = sb("wi_lo", [P, KC, E * F], F32R)
        wo = sb("wo", [P, FC, D])
        wo_hi = sb("wo_hi", [P, FC, D], F32R)
        wo_lo = sb("wo_lo", [P, FC, D], F32R)
        x_sb = sb("x_sb", [P, 2, TILES, D])
        ctx_t_sb = sb("ctx_t_sb", [P, 2, KC, 4 * S])
        ctx_sb = sb("ctx_sb", [P, 2, 2, D])
        stats = sb("stats", [P, TILES, 6])
        mean_var = sb("mean_var", [P, TILES, 2])
        var_eps = sb("var_eps", [P, TILES])
        rstd = sb("rstd", [P, TILES])
        xc = sb("xc", [P, TILES, D])
        xc_t = sb("xc_t", [P, TILES, KC, P])
        masked = sb("masked", [P, TILES, S])
        row_max = sb("row_max", [P, TILES])
        centred = sb("centred", [P, TILES, S])
        probs = sb("probs", [P, TILES, S])
        probs_t = sb("probs_t", [P, P])
        row_sum = sb("row_sum", [P, TILES])
        row_inv = sb("row_inv", [P, TILES])
        row_scale = sb("row_scale", [P, TILES])
        x2 = sb("x2", [P, 2, TILES, D])
        stats2 = sb("stats2", [P, TILES, 6])
        mean_var2 = sb("mean_var2", [P, TILES, 2])
        var_eps2 = sb("var_eps2", [P, TILES])
        minus_mean = sb("minus_mean", [P, TILES])
        minus_mean2 = sb("minus_mean2", [P, TILES])
        rstd2 = sb("rstd2", [P, TILES])
        x2n = sb("x2n", [P, 2, TILES, D])
        x2t_hi = sb("x2t_hi", [P, 2, KC, GROUP], F32R)
        x2t_lo = sb("x2t_lo", [P, 2, KC, GROUP], F32R)
        gate_prod = sb("gate_prod", [P, TILES, D])
        gate_sum = sb("gate_sum", [P, TILES])
        chosen = sb("chosen", [P, 2, E, TILES])
        bias0 = sb("bias0", [P, TILES, D])
        bias1 = sb("bias1", [P, TILES, D])
        bias01 = sb("bias01", [P, TILES, D])
        base = sb("base", [P, 2, TILES, D])
        hid = sb("hid", [P, 2, CS, GROUP])
        hid_hi = sb("hid_hi", [P, STEPS, CS, GROUP], F32R)
        hid_lo = sb("hid_lo", [P, STEPS, CS, GROUP], F32R)
        part = sb("part", [P, TILES, D])
        out_sb = sb("out_sb", [P, 2, TILES, D])

        ps_hid = [bank(f"ps_hid{i}") for i in range(2)]
        ps_y = [bank(f"ps_y{e}") for e in range(E)]
        ps_read = [bank(f"ps_read{j}") for j in range(2)]
        ps_turn = bank("ps_turn")
        ps_score = bank("ps_score")
        ps_xc = (ps_turn, ps_score)

        ps_last = ps_hid[0][:, 0:D]

        x0_loaded = sem("x0_loaded")
        x_loaded = [sem(f"x_loaded{i}") for i in range(2)]
        ctx_t_loaded = [sem(f"ctx_t_loaded{i}") for i in range(2)]
        ctx_loaded = [sem(f"ctx_loaded{i}") for i in range(2)]
        stored = [sem(f"stored{i}") for i in range(2)]
        mask_loaded = sem("mask_loaded")
        rows_loaded = sem("rows_loaded")
        b_in_loaded = sem("b_in_loaded")
        wi_loaded = sem("wi_loaded")
        wo_loaded = [sem(f"wo_loaded{e}") for e in range(E)]
        ident_zero = sem("ident_zero")
        ident_ready = sem("ident_ready")
        zeros_ready = sem("zeros_ready")
        consts_ready = sem("consts_ready")
        penalty_ready = sem("penalty_ready")
        gate_ready = sem("gate_ready")
        wi_hi_ready = sem("wi_hi_ready")
        wi_lo_ready = sem("wi_lo_ready")
        wi_lo2_ready = sem("wi_lo2_ready")
        wo_hi_ready = sem("wo_hi_ready")
        wo_lo_ready = sem("wo_lo_ready")
        wo_lo1_ready = sem("wo_lo1_ready")
        dve_passed, pe_passed, pool_passed = sem("dve_passed"), sem("pe_passed"), sem("pool_passed")
        stats_done = sem("stats_done")
        xc_turned = sem("xc_turned")
        x2_done = sem("x2_done")
        stats2_done = sem("stats2_done")
        xc_done = sem("xc_done")
        read_done = sem("read_done")
        x2n_done = sem("x2n_done")
        x2_turned = sem("x2_turned")
        aggr_done = sem("aggr_done")
        var_done = sem("var_done")
        rstd_done = sem("rstd_done")
        xc_t_done = sem("xc_t_done")
        scores_done = sem("scores_done")
        masked_done = sem("masked_done")
        max_done = sem("max_done")
        centred_done = sem("centred_done")
        probs_done = sem("probs_done")
        probs_turned = sem("probs_turned")
        probs_t_done = sem("probs_t_done")
        sum_done = sem("sum_done")
        inv_done = sem("inv_done")
        scale_done = sem("scale_done")
        aggr2_done = sem("aggr2_done")
        var2_done = sem("var2_done")
        rstd2_done = sem("rstd2_done")
        x2t_hi_done = sem("x2t_hi_done")
        x2t_lo_done = sem("x2t_lo_done")
        gate_done = sem("gate_done")
        chosen_done = sem("chosen_done")
        biased = sem("biased")
        bias_sum = sem("bias_sum")
        base_done = sem("base_done")
        part_done = sem("part_done")
        out_done = sem("out_done")
        tail_done = sem("tail_done")
        tail_out_done = sem("tail_out_done")
        tail_stored = sem("tail_stored")
        hid_ready = sem("hid_ready")
        hid_taken = sem("hid_taken")
        hid_hi_done = sem("hid_hi_done")
        hid_lo_done = sem("hid_lo_done")
        second_done = sem("second_done")

        block = stack.enter_context(nc.Block())

        def run(engine, before, body):
            before()
            body(Group(0, 0), first=True)
            with engine.Fori(0, (GROUPS - 4) // 2) as pair:
                body(Group(pair, 1))
                body(Group(pair, 2))
            body(Group(0, GROUPS - 3), left=2)
            body(Group(0, GROUPS - 2), left=1)
            body(Group(0, GROUPS - 1), left=0)

        @block.sync
        def _(sp):
            def load_x(g, again=True):
                if again:
                    sp.wait_ge(x2_done, (g.n - 1) * TILES)
                sp.dma_start(x_sb[:, g.buf], x_tok[g.n]).then_inc(x_loaded[g.buf], 16)

            def load_ctx_t(g, again=True):
                if again:
                    sp.wait_ge(scores_done, g.n - 1)
                sp.dma_start(ctx_t_sb[:, g.buf], ctx_t[g.n]).then_inc(ctx_t_loaded[g.buf], 16)

            def load_ctx(g, again=True):
                if again:
                    sp.wait_ge(read_done, (g.n - 1) * TILES)
                sp.dma_start(ctx_sb[:, g.buf], ctx[g.n]).then_inc(ctx_loaded[g.buf], 16)

            def before():
                g0, g1 = Group(0, 0), Group(0, 1)
                sp.dma_start(x_sb[:, 0, 0], x_tok[0, :, 0]).then_inc(x0_loaded, 16)
                sp.dma_start(x_sb[:, 0, 1], x_tok[0, :, 1]).then_inc(x_loaded[0], 16)
                for i in range(2):
                    sp.sem_inc(stored[i], 16)
                for h in range(2):
                    sp.dma_start(mask_u8[h * S:(h + 1) * S], mask[h:h + 1].to_broadcast([S, B // 2, S])
                                 ).then_inc(mask_loaded, 16)
                load_ctx_t(g0, False)
                load_ctx(g0, False)
                load_x(g1, False)
                sp.dma_start(wi[:, :, :], w_in).then_inc(wi_loaded, 16)
                sp.dma_start(b_in_sb[:, :], b_in).then_inc(b_in_loaded, 16)
                load_ctx_t(g1, False)
                for e in (1, 0):
                    chunks = slice(e * FC // E, (e + 1) * FC // E)
                    sp.dma_start(wo[:, chunks], w_out[:, chunks]).then_inc(wo_loaded[e], 16)
                load_ctx(g1, False)
                load_x(Group(0, 2))
                sp.dma_start(gate_rows[:, :, :], gate_w.to_broadcast([P, E, D])).then_inc(rows_loaded, 16)
                sp.dma_start(b_out_sb[:, :, :], b_out.to_broadcast([P, E, D])).then_inc(rows_loaded, 16)

            def store(g):
                sp.wait_ge(out_done, g.n + 1)
                sp.dma_start(out_tok[g.n], out_sb[:, g.buf]).then_inc(stored[g.buf], 16)

            def body(g, first=False, left=3):
                if left >= 2:
                    load_ctx_t(g + 2)
                    load_ctx(g + 2)
                if left >= 3:
                    load_x(g + 3)
                if not first:
                    store(g + -1)

            run(sp, before, body)
            for t in range(TILES):
                sp.wait_ge(tail_out_done, t + 1)
                sp.dma_start(out_tok[GROUPS - 1, :, t], out_sb[:, (GROUPS - 1) % 2, t]).then_inc(tail_stored, 16)
            sp.wait_ge(stored[0], 16 * (GROUPS // 2 + 1))
            sp.wait_ge(stored[1], 16 * (GROUPS // 2))
            sp.wait_ge(tail_stored, 16 * TILES)

        @block.gpsimd
        def _(pool):
            def first_norm(g):
                pool.wait_ge(rstd_done, g.n)
                pool.wait_ge(aggr_done, g.n + 1)
                pool.tensor_tensor(minus_mean[:, :], mean_var[:, :, 0], minus_one[:, :], ALU.mult)
                pool.tensor_tensor(var_eps[:, :], mean_var[:, :, 1], eps[:, :], ALU.add).then_inc(var_done, 1)
                pool.wait_ge(var_done, g.n + 1)
                pool.wait_ge(xc_turned, g.n * TILES)
                pool.sem_inc(pool_passed, 1)
                for t in range(TILES):
                    pool.tensor_scalar(xc[:, t], x_sb[:, g.buf, t], minus_mean[:, t:t + 1], 1.0,
                                       ALU.add, ALU.mult).then_inc(xc_done, 1)
                pool.wait_ge(masked_done, g.n)
                pool.tensor_tensor(rstd[:, :], var_eps[:, :], minus_half[:, :], ALU.pow).then_inc(rstd_done, 1)

            def second_norm(g):
                if not (isinstance(g.n, int) and g.n < 2):
                    pool.wait_ge(x2_turned, (g.n - 1) * TILES)
                    pool.wait_ge(gate_done, g.n - 1)
                pool.wait_ge(aggr2_done, g.n + 1)
                pool.tensor_tensor(var_eps2[:, :], mean_var2[:, :, 1], eps[:, :], ALU.add).then_inc(var2_done, 1)
                pool.tensor_tensor(minus_mean2[:, :], mean_var2[:, :, 0], minus_one[:, :], ALU.mult)
                pool.wait_ge(var2_done, g.n + 1)
                pool.tensor_tensor(rstd2[:, :], var_eps2[:, :], minus_half[:, :], ALU.pow).then_inc(rstd2_done, 1)
                pool.wait_ge(rstd2_done, g.n + 1)
                pool.sem_inc(pool_passed, 1)
                for t in range(TILES):
                    pool.tensor_scalar(x2n[:, g.buf, t], x2[:, g.buf, t], minus_mean2[:, t:t + 1],
                                       rstd2[:, t:t + 1], ALU.add, ALU.mult).then_inc(x2n_done, 1)

            def choose_bias(g):
                pool.wait_ge(chosen_done, g.n + 1)
                pool.sem_inc(pool_passed, 1)
                for t in range(TILES):
                    pool.tensor_scalar(bias0[:, t], b_out_sb[:, 0], chosen[:, g.buf, 0, t:t + 1], 0.0,
                                       ALU.mult, ALU.add)
                    last = pool.tensor_scalar(bias1[:, t], b_out_sb[:, 1], chosen[:, g.buf, 1, t:t + 1], 0.0,
                                              ALU.mult, ALU.add)
                last.then_inc(biased, 1)

            def residual(g):
                pool.wait_ge(biased, g.n + 1)
                pool.tensor_tensor(bias01[:, :, :], bias0[:, :, :], bias1[:, :, :], ALU.add).then_inc(bias_sum, 1)
                pool.wait_ge(bias_sum, g.n + 1)
                pool.tensor_tensor(base[:, g.buf], bias01[:, :, :], x2[:, g.buf], ALU.add).then_inc(base_done, 1)

            def before():
                pool.memset(ident[:, :], 0.0).then_inc(ident_zero, 1)
                for const, value in ((minus_half, -0.5), (minus_one, -1.0), (eps, EPS)):
                    pool.memset(const[:, :], value).then_inc(consts_ready, 1)
                pool.wait_ge(ident_zero, 1)
                pool.affine_select(out=ident[:, :], in_=ident[:, :], compare_op=ALU.not_equal, fill=1.0, base=0,
                                   pattern=[[-1, P]], channel_multiplier=1).then_inc(ident_ready, 1)
                pool.wait_ge(consts_ready, 3)
                pool.wait_ge(var_done, 1)
                pool.tensor_tensor(rstd[:, :], var_eps[:, :], minus_half[:, :], ALU.pow).then_inc(rstd_done, 1)
                first_norm(Group(0, 1))
                pool.wait_ge(var2_done, 1)
                pool.tensor_tensor(rstd2[:, :], var_eps2[:, :], minus_half[:, :], ALU.pow).then_inc(rstd2_done, 1)

                def out_lo(q, nth):
                    pool.wait_ge(wo_hi_ready, nth)
                    chunk = slice(q * CS, (q + 1) * CS)
                    pool.tensor_tensor(wo_lo[:, chunk], wo[:, chunk], wo_hi[:, chunk].bitcast(F32),
                                       ALU.subtract).then_inc(wo_lo_ready, 1)

                pool.wait_ge(wi_hi_ready, 3)
                cols = slice(2 * CS * P, 3 * CS * P)
                pool.tensor_tensor(wi_lo[:, :, cols], wi[:, :, cols], wi_hi[:, :, cols].bitcast(F32),
                                   ALU.subtract).then_inc(wi_lo2_ready, 1)
                out_lo(2, 1)
                out_lo(0, 3)
                first_norm(Group(0, 2))
                second_norm(Group(0, 1))
                out_lo(3, 2)
                pool.wait_ge(rows_loaded, 32)

            def body(g, first=False, left=3):
                if left >= 2 and not first:
                    first_norm(g + 2)
                choose_bias(g)
                if left >= 1 and not first:
                    second_norm(g + 1)
                residual(g)

            run(pool, before, body)

        @block.scalar
        def _(act):
            def keep_xc_t(g):
                for t in range(TILES):
                    act.wait_ge(xc_turned, g.n * TILES + t + 1)
                    last = act.copy(xc_t[:, t], ps_xc[t][:, 0:D])
                last.then_inc(xc_t_done, 1)

            def exps(g):
                act.wait_ge(centred_done, g.n + 1)
                act.activation(probs[:, :, :], centred[:, :, :], ACT.Exp, scale=float(D) ** -0.5
                               ).then_inc(probs_done, 1)

            def keep_probs_t(g):
                act.wait_ge(probs_turned, g.n + 1)
                act.copy(probs_t[:, :], ps_turn[:, 0:P]).then_inc(probs_t_done, 1)

            def keep_x2t(g):
                for t in range(TILES):
                    act.wait_ge(x2_turned, g.n * TILES + t + 1)
                    last = act.copy(x2t_hi[:, g.buf, :, t * P:(t + 1) * P],
                                    ps_read[t][:, 0:D].rearrange("p (k n) -> p k n", k=KC))
                last.then_inc(x2t_hi_done, 1)

            def hidden(g, q):
                n = g.n * STEPS + q
                if not (isinstance(g.n, int) and n < 2):
                    act.wait_ge(hid_lo_done, n - 1)
                act.wait_ge(hid_ready, n + 1)
                for c in range(CS):
                    chunk = q * CS + c
                    last = act.activation(hid[:, q % 2, c], ps_hid[q % 2][:, c * GROUP:(c + 1) * GROUP],
                                          ACT.Gelu if chunk < FC // E else ACT.Relu,
                                          bias=b_in_sb[:, chunk:chunk + 1])
                last.then_inc(hid_taken, 1)
                act.wait_ge(hid_taken, n + 1)
                act.copy(hid_hi[:, q], hid[:, q % 2]).then_inc(hid_hi_done, 1)

            def out_hi(q):
                chunk = slice(q * CS, (q + 1) * CS)
                act.copy(wo_hi[:, chunk], wo[:, chunk]).then_inc(wo_hi_ready, 1)

            def before():
                g0, g1 = Group(0, 0), Group(0, 1)

                def in_hi(q):
                    cols = slice(q * CS * P, (q + 1) * CS * P)
                    act.copy(wi_hi[:, :, cols], wi[:, :, cols]).then_inc(wi_hi_ready, 1)

                keep_xc_t(g0)
                exps(g0)
                keep_probs_t(g0)
                act.wait_ge(wi_loaded, 16)
                in_hi(0)
                in_hi(1)
                keep_xc_t(g1)
                in_hi(2)
                in_hi(3)
                act.wait_ge(wo_loaded[1], 16)
                out_hi(2)
                out_hi(3)
                keep_x2t(g0)
                exps(g1)
                act.wait_ge(b_in_loaded, 16)
                act.wait_ge(wo_loaded[0], 16)
                out_hi(0)
                keep_probs_t(g1)
                act.wait_ge(consts_ready, 3)
                act.activation(unused[:, :], minus_one[:, :], ACT.Gelu)

            def body(g, first=False, left=3):
                hidden(g, 0)
                hidden(g, 1)
                if left >= 2:
                    keep_xc_t(g + 2)
                if first:
                    out_hi(1)
                hidden(g, 2)
                if left >= 1:
                    keep_x2t(g + 1)
                if left >= 2:
                    exps(g + 2)
                hidden(g, 3)
                if left >= 2:
                    keep_probs_t(g + 2)

            run(act, before, body)

        @block.vector
        def _(dve):
            def norm_stats(g, src, stats, mean_var, stats_done, aggr_done, await_tile=lambda t: None):
                for t in range(TILES):
                    await_tile(t)
                    dve.bn_stats(stats[:, t], src[:, t]).then_inc(stats_done, 1)
                for t in range(TILES):
                    dve.wait_ge(stats_done, g.n * TILES + t + 1)
                    if not isinstance(g.n, int):
                        dve.sem_inc(dve_passed, 1)
                    last = dve.bn_aggr(mean_var[:, t], stats[:, t])
                last.then_inc(aggr_done, 1)

            def first_stats(g):
                dve.wait_ge(xc_done, g.n * TILES)
                dve.wait_ge(x_loaded[g.buf], 16 * (g.turn + 1))
                norm_stats(g, x_sb[:, g.buf], stats, mean_var, stats_done, aggr_done)

            def mask_scores(g):
                dve.wait_ge(scores_done, g.n + 1)
                dve.wait_ge(rstd_done, g.n + 1)
                for t in range(TILES):
                    last = dve.scalar_tensor_tensor(out=masked[:, t], in0=ps_score[:, t * S:(t + 1) * S],
                                                    scalar=rstd[:, t:t + 1], in1=penalty[:, g.n * TILES + t],
                                                    op0=ALU.mult, op1=ALU.add)
                last.then_inc(masked_done, 1)
                dve.wait_ge(masked_done, g.n + 1)
                dve.tensor_reduce(row_max[:, :], masked[:, :, :], AX_X, ALU.max).then_inc(max_done, 1)
                dve.wait_ge(max_done, g.n + 1)
                dve.tensor_tensor(centred[:, :, :], masked[:, :, :],
                                  row_max[:, :].unsqueeze(2).to_broadcast([P, TILES, S]),
                                  ALU.subtract).then_inc(centred_done, 1)

            def sum_probs(g):
                dve.wait_ge(probs_done, g.n + 1)
                dve.tensor_reduce(row_sum[:, :], probs[:, :, :], AX_X, ALU.add).then_inc(sum_done, 1)
                dve.wait_ge(sum_done, g.n + 1)
                dve.reciprocal(row_inv[:, :], row_sum[:, :]).then_inc(inv_done, 1)
                dve.wait_ge(inv_done, g.n + 1)
                dve.scalar_tensor_tensor(out=row_scale[:, :], in0=row_max[:, :], scalar=0.1 * NEG,
                                         in1=row_inv[:, :], op0=ALU.is_gt, op1=ALU.mult).then_inc(scale_done, 1)

            def add_readout(g):
                if not (isinstance(g.n, int) and g.n < 2):
                    dve.wait_ge(base_done, g.n - 1)
                dve.wait_ge(scale_done, g.n + 1)
                for t in range(TILES):
                    dve.wait_ge(read_done, g.n * TILES + t + 1)
                    last = dve.scalar_tensor_tensor(out=x2[:, g.buf, t], in0=ps_read[t][:, 0:D],
                                                    scalar=row_scale[:, t:t + 1], in1=x_sb[:, g.buf, t],
                                                    op0=ALU.mult, op1=ALU.add)
                    last.then_inc(x2_done, 1)

            def second_stats(g):
                if not (isinstance(g.n, int) and g.n == 0):
                    dve.wait_ge(x2n_done, g.n * TILES)
                norm_stats(g, x2[:, g.buf], stats2, mean_var2, stats2_done, aggr2_done,
                           await_tile=lambda t: dve.wait_ge(x2_done, g.n * TILES + t + 1))

            def gate(g):
                if not (isinstance(g.n, int) and g.n == 0):
                    dve.wait_ge(chosen_done, g.n)
                dve.wait_ge(x2n_done, (g.n + 1) * TILES)
                for t in range(TILES):
                    last = dve.tensor_tensor_reduce(gate_prod[:, t], x2n[:, g.buf, t], gate_diff[:, :], 1.0, 0.0,
                                                    ALU.mult, ALU.add, gate_sum[:, t:t + 1])
                last.then_inc(gate_done, 1)
                dve.wait_ge(gate_done, g.n + 1)
                dve.tensor_scalar(chosen[:, g.buf, 0], gate_sum[:, :], 0.0, None, ALU.is_ge)
                dve.tensor_scalar(chosen[:, g.buf, 1], gate_sum[:, :], 0.0, None, ALU.is_lt).then_inc(chosen_done, 1)

            def x2t_low(g):
                dve.wait_ge(x2t_hi_done, g.n + 1)
                for t in range(TILES):
                    toks = slice(t * P, (t + 1) * P)
                    last = dve.tensor_tensor(x2t_lo[:, g.buf, :, toks],
                                             ps_read[t][:, 0:D].rearrange("p (k n) -> p k n", k=KC),
                                             x2t_hi[:, g.buf, :, toks].bitcast(F32), ALU.subtract)
                last.then_inc(x2t_lo_done, 1)

            def hidden_low(g, q):
                n = g.n * STEPS + q
                if not (isinstance(g.n, int) and g.n == 0):
                    dve.wait_ge(second_done, n + 1 - STEPS)
                dve.wait_ge(hid_hi_done, n + 1)
                dve.tensor_tensor(hid_lo[:, q], hid[:, q % 2], hid_hi[:, q].bitcast(F32),
                                  ALU.subtract).then_inc(hid_lo_done, 1)

            def add_expert0(g):
                if not (isinstance(g.n, int) and g.n == 0):
                    dve.wait_ge(out_done, g.n)
                dve.wait_ge(base_done, g.n + 1)
                dve.wait_ge(second_done, g.n * STEPS + 2)
                for t in range(TILES):
                    last = dve.scalar_tensor_tensor(out=part[:, t], in0=ps_y[0][:, t * D:(t + 1) * D],
                                                    scalar=chosen[:, g.buf, 0, t:t + 1], in1=base[:, g.buf, t],
                                                    op0=ALU.mult, op1=ALU.add)
                last.then_inc(part_done, 1)

            def add_expert1(g):
                dve.wait_ge(stored[g.buf], 16 * (g.turn + 1))
                dve.wait_ge(part_done, g.n + 1)
                dve.wait_ge(second_done, g.n * STEPS + 4)
                for t in range(TILES):
                    last = dve.scalar_tensor_tensor(out=out_sb[:, g.buf, t], in0=ps_y[1][:, t * D:(t + 1) * D],
                                                    scalar=chosen[:, g.buf, 1, t:t + 1], in1=part[:, t],
                                                    op0=ALU.mult, op1=ALU.add)
                last.then_inc(out_done, 1)

            def in_lo(q):
                dve.wait_ge(wi_hi_ready, q + 1)
                cols = slice(q * CS * P, (q + 1) * CS * P)
                dve.tensor_tensor(wi_lo[:, :, cols], wi[:, :, cols], wi_hi[:, :, cols].bitcast(F32),
                                  ALU.subtract).then_inc(wi_lo_ready, 1)

            def out_lo_1():
                dve.wait_ge(wo_hi_ready, STEPS)
                chunk = slice(CS, 2 * CS)
                dve.tensor_tensor(wo_lo[:, chunk], wo[:, chunk], wo_hi[:, chunk].bitcast(F32),
                                  ALU.subtract).then_inc(wo_lo1_ready, 1)

            def before():
                g0, g1 = Group(0, 0), Group(0, 1)

                dve.memset(zeros[:, :], 0.0).then_inc(zeros_ready, 1)
                norm_stats(g0, x_sb[:, 0], stats, mean_var, stats_done, aggr_done,
                           await_tile=lambda t: dve.wait_ge(x_loaded[0] if t else x0_loaded, 16))
                dve.wait_ge(aggr_done, 1)
                dve.tensor_scalar(var_eps[:, :], mean_var[:, :, 1], EPS, None, ALU.add).then_inc(var_done, 1)
                for t in range(TILES):
                    dve.tensor_scalar(xc[:, t], x_sb[:, 0, t], mean_var[:, t, 0:1], None,
                                      ALU.subtract).then_inc(xc_done, 1)
                dve.wait_ge(mask_loaded, 32)
                dve.tensor_scalar(penalty[:, :, :], mask_u8[:, :, :], -1.0, -NEG, ALU.add, ALU.mult
                                  ).then_inc(penalty_ready, 1)
                dve.wait_ge(penalty_ready, 1)
                mask_scores(g0)
                first_stats(g1)
                sum_probs(g0)
                add_readout(g0)
                second_stats(g0)
                dve.wait_ge(aggr2_done, 1)
                dve.tensor_scalar(var_eps2[:, :], mean_var2[:, :, 1], EPS, None, ALU.add).then_inc(var2_done, 1)
                in_lo(0)
                dve.wait_ge(rstd2_done, 1)
                for t in range(TILES):
                    dve.tensor_scalar(x2n[:, 0, t], x2[:, 0, t], mean_var2[:, t, 0:1], rstd2[:, t:t + 1],
                                      ALU.subtract, ALU.mult).then_inc(x2n_done, 1)
                mask_scores(g1)
                x2t_low(g0)
                in_lo(1)
                in_lo(3)
                first_stats(Group(0, 2))
                sum_probs(g1)
                add_readout(g1)
                second_stats(g1)

            def body(g, first=False, left=3):
                if not first:
                    hidden_low(g + -1, 3)
                if left >= 1 and not first:
                    sum_probs(g + 1)
                if not first:
                    add_expert0(g + -1)
                hidden_low(g, 0)
                if first:
                    dve.wait_ge(rows_loaded, 32)
                    dve.tensor_tensor(gate_diff[:, :], gate_rows[:, 0], gate_rows[:, 1], ALU.subtract
                                      ).then_inc(gate_ready, 1)
                    dve.wait_ge(gate_ready, 1)
                    gate(g)
                elif left >= 1:
                    add_readout(g + 1)
                    second_stats(g + 1)
                hidden_low(g, 1)
                if first:
                    out_lo_1()
                if not first:
                    add_expert1(g + -1)
                if left >= 2:
                    mask_scores(g + 2)
                hidden_low(g, 2)
                if left >= 1:
                    x2t_low(g + 1)
                    gate(g + 1)
                if left >= 3:
                    first_stats(g + 3)

            run(dve, before, body)
            hidden_low(Group(0, GROUPS - 1), 3)
            add_expert0(Group(0, GROUPS - 1))
            buf = (GROUPS - 1) % 2
            dve.wait_ge(stored[buf], 16 * (GROUPS // 2))
            dve.wait_ge(part_done, GROUPS)
            for t in range(TILES):
                dve.wait_ge(tail_done, t + 1)
                dve.scalar_tensor_tensor(out=out_sb[:, buf, t], in0=ps_last if t else ps_y[1][:, 0:D],
                                         scalar=chosen[:, buf, 1, t:t + 1], in1=part[:, t],
                                         op0=ALU.mult, op1=ALU.add).then_inc(tail_out_done, 1)

        @block.tensor
        def _(pe):
            def turn_xc(g):
                if not (isinstance(g.n, int) and g.n == 0):
                    pe.wait_ge(probs_t_done, g.n)
                    pe.wait_ge(masked_done, g.n)
                for t in range(TILES):
                    pe.wait_ge(xc_done, g.n * TILES + t + 1)
                    for k in range(KC):
                        last = pe.transpose(ps_xc[t][:, k * P:(k + 1) * P],
                                            xc[:, t, k * P:(k + 1) * P], ident[:, :])
                    last.then_inc(xc_turned, 1)

            def scores(g):
                pe.wait_ge(xc_t_done, g.n + 1)
                pe.wait_ge(ctx_t_loaded[g.buf], 16 * (g.turn + 1))
                for t in range(TILES):
                    for k in range(KC):
                        for h in range(2):
                            b = 2 * t + h
                            last = pe.matmul(ps_score[h * S:(h + 1) * S, t * S:(t + 1) * S],
                                             xc_t[:, t, k, h * S:(h + 1) * S],
                                             ctx_t_sb[:, g.buf, k, b * S:(b + 1) * S],
                                             start=(k == 0), stop=(k == KC - 1))
                last.then_inc(scores_done, 1)

            def turn_probs(g):
                pe.wait_ge(probs_done, g.n + 1)
                pe.transpose(ps_turn[:, 0:P], probs[:, :, :].rearrange("p t m -> p (t m)"), ident[:, :]
                             ).then_inc(probs_turned, 1)

            def readout(g):
                if not (isinstance(g.n, int) and g.n == 0):
                    pe.wait_ge(x2t_lo_done, g.n)
                pe.wait_ge(probs_t_done, g.n + 1)
                pe.wait_ge(ctx_loaded[g.buf], 16 * (g.turn + 1))
                pe.sem_inc(pe_passed, 1)
                for t in range(TILES):
                    for h in range(2):
                        last = pe.matmul(ps_read[t][h * S:(h + 1) * S, 0:D],
                                         probs_t[t * S:(t + 1) * S, h * S:(h + 1) * S],
                                         ctx_sb[t * S:(t + 1) * S, g.buf, h], start=True, stop=True)
                    last.then_inc(read_done, 1)

            def turn_x2n(g):
                for t in range(TILES):
                    pe.wait_ge(x2n_done, g.n * TILES + t + 1)
                    for k in range(KC):
                        last = pe.transpose(ps_read[t][:, k * P:(k + 1) * P],
                                            x2n[:, g.buf, t, k * P:(k + 1) * P], ident[:, :])
                    last.then_inc(x2_turned, 1)

            def first_product(g, q, first=False, midway=lambda: None):
                n = g.n * STEPS + q
                if first:
                    if q == 2:
                        pe.wait_ge(wi_lo2_ready, 1)
                    else:
                        pe.wait_ge(wi_lo_ready, min(q + 1, 3))
                if not first or q >= 2:
                    pe.wait_ge(hid_taken, n - 1)
                if q == 0:
                    pe.wait_ge(x2t_hi_done, g.n + 1)
                def dst(c):
                    return ps_hid[q % 2][:, c * GROUP:(c + 1) * GROUP]

                def cols(c):
                    return slice((q * CS + c) * P, (q * CS + c + 1) * P)

                for c in range(CS):
                    for k in range(KC):
                        hi = x2t_hi[:, g.buf, k]
                        pe.matmul(dst(c), wi_hi[:, k, cols(c)], hi, start=(c == 0 and k == 0), stop=False,
                                  skip_group_check=True)
                        pe.matmul(dst(c), wi_lo[:, k, cols(c)], hi, start=False, stop=False, skip_group_check=True)
                midway()
                if q == 0:
                    pe.wait_ge(x2t_lo_done, g.n + 1)
                for c in range(CS):
                    for k in range(KC):
                        last = pe.matmul(dst(c), wi_hi[:, k, cols(c)], x2t_lo[:, g.buf, k], start=False,
                                         stop=(k == KC - 1), skip_group_check=True)
                last.then_inc(hid_ready, 1)

            def second_product(g, q, first=False, tail=False):
                n = g.n * STEPS + q
                e = q * CS // (FC // E)
                if first:
                    if q == 0:
                        pe.wait_ge(wo_lo_ready, 2)
                    else:
                        pe.wait_ge(wo_lo_ready, 3)
                        pe.wait_ge(wo_lo1_ready, 1)
                elif q == 0:
                    pe.wait_ge(part_done, g.n)
                elif q == STEPS // 2:
                    pe.wait_ge(out_done, g.n)
                pe.wait_ge(hid_hi_done, n + 1)
                if tail:
                    pe.wait_ge(hid_taken, GROUPS * STEPS - 1)

                def dst(t):
                    return ps_last if tail and t else ps_y[e][:, t * D:(t + 1) * D]

                for tiles in [(t,) for t in range(TILES)] if tail else [range(TILES)]:
                    for c in range(CS):
                        for t in tiles:
                            chunk, toks = q * CS + c, slice(t * P, (t + 1) * P)
                            opens = chunk % (FC // E) == 0 and (t == 0 or tail)
                            pe.matmul(dst(t), hid_hi[:, q, c, toks], wo_hi[:, chunk], start=opens, stop=False,
                                      skip_group_check=True)
                            pe.matmul(dst(t), hid_hi[:, q, c, toks], wo_lo[:, chunk], start=False, stop=False,
                                      skip_group_check=True)
                    pe.wait_ge(hid_lo_done, n + 1)
                    for c in range(CS):
                        for t in tiles:
                            chunk, toks = q * CS + c, slice(t * P, (t + 1) * P)
                            closes = chunk % (FC // E) == FC // E - 1
                            last = pe.matmul(dst(t), hid_lo[:, q, c, toks], wo_hi[:, chunk], start=False,
                                             stop=closes, skip_group_check=True)
                    if tail and closes:
                        last.then_inc(tail_done, 1)
                if not tail:
                    last.then_inc(second_done, 1)

            def before():
                g0, g1 = Group(0, 0), Group(0, 1)

                def keep_warm(count):
                    for _ in range(count):
                        pe.matmul(ps_y[1][:, 0:P], zeros[:, :], zeros[:, :], start=True, stop=True)

                pe.wait_ge(zeros_ready, 1)
                keep_warm(34)
                pe.wait_ge(ident_ready, 1)
                turn_xc(g0)
                keep_warm(5)
                scores(g0)
                keep_warm(16)
                turn_probs(g0)
                keep_warm(6)
                readout(g0)
                turn_xc(g1)
                keep_warm(8)
                scores(g1)
                keep_warm(10)
                turn_x2n(g0)
                keep_warm(5)

            def body(g, first=False, left=3):
                if first:
                    first_product(g, 0, first, midway=lambda: turn_probs(g + 1))
                else:
                    first_product(g, 0)
                    second_product(g + -1, 2)
                if left >= 1:
                    readout(g + 1)
                first_product(g, 1, first)
                if not first:
                    second_product(g + -1, 3)
                if left >= 2 and not first:
                    turn_xc(g + 2)
                first_product(g, 2, first)
                if first:
                    turn_xc(g + 2)
                second_product(g, 0, first)
                if left >= 2:
                    scores(g + 2)
                if left >= 2:
                    turn_x2n(g + 1)
                first_product(g, 3, first)
                if left == 1:
                    turn_x2n(g + 1)
                second_product(g, 1, first)
                if left >= 2:
                    turn_probs(g + 2)

            run(pe, before, body)
            second_product(Group(0, GROUPS - 1), 2, tail=True)
            second_product(Group(0, GROUPS - 1), 3, tail=True)


def kernel(x, ctx_2048, mask_BxS2_bk0, L0_ffn_Wg, L0_ffn_W0a, L0_ffn_b0a, L0_ffn_W0b, L0_ffn_b0b,
           L0_ffn_W1a, L0_ffn_b1a, L0_ffn_W1b, L0_ffn_b1b):
    import numpy as np
    import concourse.bacc as bacc
    from concourse.bass_utils import run_bass_kernel_spmd

    ctx_np = np.asarray(ctx_2048)
    ctx_t = ctx_np.reshape(GROUPS, 4, S, KC, P).transpose(0, 4, 3, 1, 2).reshape(GROUPS, P, KC, 4 * S)
    ctx = ctx_np.reshape(GROUPS, TILES, 2, S, D).transpose(0, 1, 3, 2, 4).reshape(GROUPS, P, 2, D)
    mask = np.asarray(mask_BxS2_bk0).reshape(B // 2, 2, S).transpose(1, 0, 2)
    w_in = np.concatenate([np.asarray(L0_ffn_W0a), np.asarray(L0_ffn_W1a)]).reshape(E * F, KC, P).transpose(2, 1, 0)
    b_in = np.concatenate([np.asarray(L0_ffn_b0a), np.asarray(L0_ffn_b1a)]).reshape(FC, P).T
    w_out = np.concatenate([np.asarray(L0_ffn_W0b).T, np.asarray(L0_ffn_W1b).T]).reshape(FC, P, D).transpose(1, 0, 2)
    b_out = np.stack([np.asarray(L0_ffn_b0b), np.asarray(L0_ffn_b1b)])[None]
    gate_w = np.asarray(L0_ffn_Wg)[None]
    arrays = {
        "x": np.asarray(x).reshape(B * S, D), "ctx": ctx, "ctx_t": ctx_t, "mask": mask, "gate_w": gate_w,
        "w_in": w_in, "b_in": b_in, "w_out": w_out, "b_out": b_out,
    }
    arrays = {name: np.ascontiguousarray(a) for name, a in arrays.items()}

    nc = bacc.Bacc("TRN2", target_bir_lowering=False, num_devices=1)
    aps = {name: nc.dram_tensor(name, a.shape, mybir.dt.from_np(a.dtype), kind="ExternalInput").ap()
           for name, a in arrays.items()}
    aps["out"] = nc.dram_tensor("out", (B * S, D), F32, kind="ExternalOutput").ap()
    xattn_ffn(nc, **aps)
    result = run_bass_kernel_spmd(nc, [arrays], core_ids=[0])
    return result.results[0]["out"].reshape(B, S, D)
```
